# Optimizing a Trainium2 kernel written in Bass

```python
import numpy as np
import jax
import jax.numpy as jnp

def _softmax(x, axis=-1):
    return jax.nn.softmax(x, axis=axis)

def _gelu(x):
    return jax.nn.gelu(x, approximate=True)

def _silu(x):
    return jax.nn.silu(x)

def _sigmoid(x):
    return jax.nn.sigmoid(x)

def _layernorm(x, axis=-1, eps=1e-05):
    m = jnp.mean(x, axis=axis, keepdims=True)
    v = jnp.var(x, axis=axis, keepdims=True)
    return (x - m) / jnp.sqrt(v + eps)

def _scatter_add(tgt, idx, src, axis=0):
    return tgt.at[idx].add(src)

def _segment_sum(src, seg, n):
    return jax.ops.segment_sum(src, seg, n)
kernel_name = 'mk_recurrent_d1_jaxref_r8_5cf872'

def setup_inputs(seed: int=0):
    np.random.seed(seed)
    _w = jnp.asarray

    def _L0_attn_setup():
        import jax, jax.numpy as jnp
        import numpy as np
        NHEADS = 16
        SCALE_BASE = 64
        GN_EPS = 1e-05

        def rotate_every_two(x):
            x1 = x[..., ::2]
            x2 = x[..., 1::2]
            return jnp.stack((-x2, x1), axis=-1).reshape(x.shape)

        def xpos_apply(x, downscale, offset=0):
            B, T, C = x.shape
            half = C // 2
            scale_vec = (jnp.arange(0, C, 2, dtype=jnp.float32) + 0.4 * C) / (1.4 * C)
            min_pos = -(T + offset) // 2
            max_pos = T + offset + min_pos
            power = jnp.arange(min_pos, max_pos, dtype=jnp.float32) / SCALE_BASE
            scale = scale_vec[None, :] ** power[:, None]
            L = scale.shape[0]
            inv_freq = 1.0 / 10000.0 ** (jnp.arange(half, dtype=jnp.float32) / half)
            sinusoid = jnp.arange(L, dtype=jnp.float32)[:, None] * inv_freq[None, :]
            sin, cos = (jnp.sin(sinusoid), jnp.cos(sinusoid))
            if L > T:
                scale, sin, cos = (scale[-T:], sin[-T:], cos[-T:])
            if downscale:
                scale = 1.0 / scale
            sin = jnp.repeat(sin * scale, 2, axis=-1)
            cos = jnp.repeat(cos * scale, 2, axis=-1)
            return x * cos + rotate_every_two(x) * sin

        def decay_mask(nheads, T):
            gamma = 1.0 - 2.0 ** (-5.0 - jnp.arange(nheads, dtype=jnp.float32))
            idx = jnp.arange(T)
            diff = idx[:, None] - idx[None, :]
            keep = diff >= 0
            m = gamma[:, None, None] ** jnp.where(keep, diff, 0).astype(jnp.float32)
            return jnp.where(keep[None, :, :], m, 0.0)
        key = jax.random.key(seed)
        ks = jax.random.split(key, 6)
        B, T, C = (2, 256, 128)
        w_std = 0.02
        return {'x': jax.random.normal(ks[0], (B, T, C), jnp.float32), 'w_qkvff': jax.random.normal(ks[1], (5 * C, C), jnp.float32) * w_std, 'w_gated': jax.random.normal(ks[2], (C, C), jnp.float32) * w_std, 'b_gated': jnp.zeros((C,), jnp.float32), 'w_proj': jax.random.normal(ks[3], (C, C), jnp.float32) * w_std, 'b_proj': jnp.zeros((C,), jnp.float32), 'gn_w': jnp.ones((C,), jnp.float32), 'gn_b': jnp.zeros((C,), jnp.float32), 'w_ff': jax.random.normal(ks[4], (C, 2 * C), jnp.float32) * w_std, 'rms_w': jnp.ones((C,), jnp.float32)}
    _L0_attn_in = _L0_attn_setup()

    def _L0_ffn_setup():
        import jax, jax.numpy as jnp
        import numpy as np
        TOP_K = 4
        N_GROUP = 4
        TOPK_GROUP = 2
        ROUTED_SCALING = 2.5

        def _route(x, gate_weight):
            scores = jax.nn.sigmoid(x @ gate_weight.T)
            T, E = scores.shape
            gs = E // N_GROUP
            top2, _ = jax.lax.top_k(scores.reshape(T, N_GROUP, gs), 2)
            group_scores = top2.sum(-1)
            _, gidx = jax.lax.top_k(group_scores, TOPK_GROUP)
            gmask = jax.nn.one_hot(gidx, N_GROUP, dtype=jnp.float32).sum(1)
            smask = jnp.repeat(gmask, gs, axis=1) > 0.5
            masked = jnp.where(smask, scores, 0.0)
            topk_idx = jax.lax.top_k(masked, TOP_K)[1]
            topk_w = jnp.take_along_axis(scores, topk_idx, axis=1)
            topk_w = topk_w / (topk_w.sum(-1, keepdims=True) + 1e-20)
            topk_w = topk_w * ROUTED_SCALING
            combine = jnp.zeros((T, E), jnp.float32).at[jnp.arange(T)[:, None], topk_idx].add(topk_w)
            return combine
        key = jax.random.key(seed)
        ks = jax.random.split(key, 6)
        B, S, H = (2, 128, 128)
        E, I, Is = (16, 64, 256)
        g = lambda k, shape, scale: jax.random.normal(k, shape, dtype=jnp.float32) * scale
        return {'hidden_states': g(ks[0], (B, S, H), 1.0), 'gate_weight': g(ks[1], (E, H), 0.02), 'expert_up': g(ks[2], (E, H, I), 0.02), 'expert_down': g(ks[3], (E, I, H), 0.02), 'shared_up': g(ks[4], (H, Is), 0.02), 'shared_down': g(ks[5], (Is, H), 0.02)}
    _L0_ffn_in = _L0_ffn_setup()
    _d = {'L0_attn_x': _L0_attn_in['x'], 'L0_attn_w_qkvff': _L0_attn_in['w_qkvff'], 'L0_attn_w_gated': _L0_attn_in['w_gated'], 'L0_attn_b_gated': _L0_attn_in['b_gated'], 'L0_attn_w_proj': _L0_attn_in['w_proj'], 'L0_attn_b_proj': _L0_attn_in['b_proj'], 'L0_attn_gn_w': _L0_attn_in['gn_w'], 'L0_attn_gn_b': _L0_attn_in['gn_b'], 'L0_attn_w_ff': _L0_attn_in['w_ff'], 'L0_attn_rms_w': _L0_attn_in['rms_w'], 'L0_ffn_gate_weight': _L0_ffn_in['gate_weight'], 'L0_ffn_expert_up': _L0_ffn_in['expert_up'], 'L0_ffn_expert_down': _L0_ffn_in['expert_down'], 'L0_ffn_shared_up': _L0_ffn_in['shared_up'], 'L0_ffn_shared_down': _L0_ffn_in['shared_down']}
    _x0 = _d['L0_attn_x']
    _d['L0_attn_x'] = jax.random.normal(jax.random.fold_in(jax.random.key(seed), 1), (16, 512, 128), dtype=_x0.dtype)
    del _x0
    return _d

def reference(L0_attn_x, L0_attn_w_qkvff, L0_attn_w_gated, L0_attn_b_gated, L0_attn_w_proj, L0_attn_b_proj, L0_attn_gn_w, L0_attn_gn_b, L0_attn_w_ff, L0_attn_rms_w, L0_ffn_gate_weight, L0_ffn_expert_up, L0_ffn_expert_down, L0_ffn_shared_up, L0_ffn_shared_down):

    def _L0_attn_ref(x, w_qkvff, w_gated, b_gated, w_proj, b_proj, gn_w, gn_b, w_ff, rms_w):
        import jax, jax.numpy as jnp
        import numpy as np
        NHEADS = 16
        SCALE_BASE = 64
        GN_EPS = 1e-05

        def rotate_every_two(x):
            x1 = x[..., ::2]
            x2 = x[..., 1::2]
            return jnp.stack((-x2, x1), axis=-1).reshape(x.shape)

        def xpos_apply(x, downscale, offset=0):
            B, T, C = x.shape
            half = C // 2
            scale_vec = (jnp.arange(0, C, 2, dtype=jnp.float32) + 0.4 * C) / (1.4 * C)
            min_pos = -(T + offset) // 2
            max_pos = T + offset + min_pos
            power = jnp.arange(min_pos, max_pos, dtype=jnp.float32) / SCALE_BASE
            scale = scale_vec[None, :] ** power[:, None]
            L = scale.shape[0]
            inv_freq = 1.0 / 10000.0 ** (jnp.arange(half, dtype=jnp.float32) / half)
            sinusoid = jnp.arange(L, dtype=jnp.float32)[:, None] * inv_freq[None, :]
            sin, cos = (jnp.sin(sinusoid), jnp.cos(sinusoid))
            if L > T:
                scale, sin, cos = (scale[-T:], sin[-T:], cos[-T:])
            if downscale:
                scale = 1.0 / scale
            sin = jnp.repeat(sin * scale, 2, axis=-1)
            cos = jnp.repeat(cos * scale, 2, axis=-1)
            return x * cos + rotate_every_two(x) * sin

        def decay_mask(nheads, T):
            gamma = 1.0 - 2.0 ** (-5.0 - jnp.arange(nheads, dtype=jnp.float32))
            idx = jnp.arange(T)
            diff = idx[:, None] - idx[None, :]
            keep = diff >= 0
            m = gamma[:, None, None] ** jnp.where(keep, diff, 0).astype(jnp.float32)
            return jnp.where(keep[None, :, :], m, 0.0)
        B, T, C = x.shape
        H = NHEADS
        hd = C // H
        nrm = jnp.sqrt(jnp.sum(x * x, axis=-1, keepdims=True)) * C ** (-0.5)
        x_ = x / jnp.maximum(nrm, 1e-08) * rms_w
        qkvff = jnp.einsum('btc,oc->bto', x_, w_qkvff)
        q, k, v, ff = jnp.split(qkvff, [C, 2 * C, 3 * C], axis=-1)
        q = xpos_apply(q, downscale=False)
        k = xpos_apply(k, downscale=True)
        q = q.reshape(B, T, H, hd).transpose(0, 2, 1, 3)
        k = k.reshape(B, T, H, hd).transpose(0, 2, 1, 3)
        v = v.reshape(B, T, H, hd).transpose(0, 2, 1, 3)
        scores = jnp.einsum('bhtd,bhsd->bhts', q, k) * hd ** (-0.5)
        scores = scores * decay_mask(H, T)[None]
        y = jnp.einsum('bhts,bhsd->bhtd', scores, v)
        yg = y.transpose(0, 2, 1, 3).reshape(B * T, H, hd)
        mu = jnp.mean(yg, axis=-1, keepdims=True)
        var = jnp.mean((yg - mu) ** 2, axis=-1, keepdims=True)
        yg = (yg - mu) / jnp.sqrt(var + GN_EPS)
        y = yg.reshape(B * T, C) * gn_w + gn_b
        y = y.reshape(B, T, C)
        y = jax.nn.silu(jnp.einsum('btc,oc->bto', x, w_gated) + b_gated) * y
        y = jnp.einsum('btc,oc->bto', y, w_proj) + b_proj
        ff_out = jnp.einsum('bte,ce->btc', jax.nn.gelu(ff, approximate=False), w_ff)
        return x + ff_out + y

    def _L0_ffn_ref(hidden_states, gate_weight, expert_up, expert_down, shared_up, shared_down):
        import jax, jax.numpy as jnp
        import numpy as np
        TOP_K = 4
        N_GROUP = 4
        TOPK_GROUP = 2
        ROUTED_SCALING = 2.5

        def _route(x, gate_weight):
            scores = jax.nn.sigmoid(x @ gate_weight.T)
            T, E = scores.shape
            gs = E // N_GROUP
            top2, _ = jax.lax.top_k(scores.reshape(T, N_GROUP, gs), 2)
            group_scores = top2.sum(-1)
            _, gidx = jax.lax.top_k(group_scores, TOPK_GROUP)
            gmask = jax.nn.one_hot(gidx, N_GROUP, dtype=jnp.float32).sum(1)
            smask = jnp.repeat(gmask, gs, axis=1) > 0.5
            masked = jnp.where(smask, scores, 0.0)
            topk_idx = jax.lax.top_k(masked, TOP_K)[1]
            topk_w = jnp.take_along_axis(scores, topk_idx, axis=1)
            topk_w = topk_w / (topk_w.sum(-1, keepdims=True) + 1e-20)
            topk_w = topk_w * ROUTED_SCALING
            combine = jnp.zeros((T, E), jnp.float32).at[jnp.arange(T)[:, None], topk_idx].add(topk_w)
            return combine
        B, S, H = hidden_states.shape
        x = hidden_states.reshape(-1, H)
        combine = _route(x.astype(jnp.float32), gate_weight)
        up = jnp.einsum('th,ehi->eti', x, expert_up)
        down = jnp.einsum('eti,eih->eth', jax.nn.silu(up), expert_down)
        moe_out = jnp.einsum('te,eth->th', combine, down)
        shared = jax.nn.silu(x @ shared_up) @ shared_down
        return (moe_out + shared).reshape(B, S, H)
    x = L0_attn_x
    xn = _layernorm(x, axis=-1)
    s = _L0_attn_ref(xn, L0_attn_w_qkvff, L0_attn_w_gated, L0_attn_b_gated, L0_attn_w_proj, L0_attn_b_proj, L0_attn_gn_w, L0_attn_gn_b, L0_attn_w_ff, L0_attn_rms_w)
    g = _silu(_L0_ffn_ref(xn, L0_ffn_gate_weight, L0_ffn_expert_up, L0_ffn_expert_down, L0_ffn_shared_up, L0_ffn_shared_down))
    x = x + s * g
    return x

_drawn_inputs = setup_inputs


def setup_inputs(seed=0):
    import zlib

    import numpy as np

    out = dict(_drawn_inputs(seed))
    spreads = {'L0_attn_b_gated': (0.0, 0.8),
     'L0_attn_b_proj': (0.0, 0.8),
     'L0_attn_gn_w': (1.0, 0.6),
     'L0_attn_gn_b': (0.0, 0.8),
     'L0_attn_rms_w': (1.0, 0.6)}
    factors = {'L0_attn_w_qkvff': 8.0,
     'L0_attn_w_gated': 8.0,
     'L0_attn_w_proj': 8.0,
     'L0_attn_w_ff': 8.0,
     'L0_ffn_gate_weight': 5.645,
     'L0_ffn_expert_up': 4.934,
     'L0_ffn_expert_down': 4.9,
     'L0_ffn_shared_up': 3.088,
     'L0_ffn_shared_down': 3.035}
    for name, (base, spread) in spreads.items():
        noise = np.random.default_rng([zlib.crc32(name.encode()), seed]).standard_normal(out[name].shape)
        drawn = base * np.exp(spread * noise) if base else spread * noise
        out[name] = jnp.asarray(drawn.astype(out[name].dtype))
    for name, factor in factors.items():
        out[name] = (out[name] * factor).astype(out[name].dtype)
    return out
```

```python
from contextlib import ExitStack

import numpy as np

import concourse.bass as bass
from concourse import mybir

P = 128
ALU = mybir.AluOpType
ACT = mybir.ActivationFunctionType
AX = mybir.AxisListType.X
F32 = mybir.dt.float32
F32R = mybir.dt.float32r

HEADS = 16
HD = 8
GROUPS = 4
CHUNK = 32
T = 512
CHUNKS = T // CHUNK
TILES = T // P
LN_EPS = 1e-5
GN_EPS = 1e-5
EXPERTS = 16
TOP_K = 4
TOPK_GROUP = 2
N_GROUP = 4
ROUTED_SCALING = 2.5

Q, QS, K, KS, V, FF, GATED, SHARED, MOE = 0, 1, 2, 3, 4, 5, 7, 8, 10
N_UP = 18
RMS_BLOCKS = 7
D_MOE, D_SHARED, D_FF, D_PROJ = 0, 8, 10, 12
N_DOWN = 13
PARTS = ((0, 0), (0, 1), (1, 0))


def shape_tables():
    C = P
    t = np.arange(T, dtype=np.float64)
    ch = np.arange(C)
    scale_vec = (np.arange(0, C, 2) + 0.4 * C) / (1.4 * C)
    power = (np.arange(T) - T // 2) / 64.0
    xpos = scale_vec[ch // 2][:, None] ** power[None, :]
    inv_freq = 1.0 / 10000.0 ** (np.arange(C // 2) / (C // 2))
    angle = t[None, :] * inv_freq[ch // 2][:, None]
    sign = np.where(ch % 2 == 0, -1.0, 1.0)[:, None]
    gamma = 1.0 - 2.0 ** (-5.0 - ch // HD)
    local = np.arange(T) % CHUNK
    grow = gamma[:, None] ** (local[None, :] + 1.0)
    cos, sin = np.cos(angle), np.sin(angle) * sign
    rope = np.stack([cos * xpos * grow * HD ** -0.5, sin * xpos * grow * HD ** -0.5,
                     cos / xpos / grow, sin / xpos / grow], 1)
    in_group = (ch // HD) % 4
    decay = gamma ** CHUNK
    col = np.arange(32)
    same_head = in_group[:, None] == (col // HD)[None, :]
    state_mask = np.repeat((same_head * decay[:, None])[:, :, None], CHUNKS, 2)
    carry = np.repeat(np.repeat(decay[:, None], 32, 1)[:, :, None], CHUNKS, 2)
    carry[:, :, 0] = 0.0
    causal = (ch % CHUNK)[:, None] <= np.arange(CHUNK)[None, :]
    head_of = in_group[:, None] == np.arange(4)[None, :]
    router = np.zeros((P, 8, P))
    for m in range(8):
        for half in range(2):
            for part in range(2):
                router[16 * part + 2 * m + half, m, 64 * half:64 * half + 64] = 1.0
    out = {
        "t_rope": rope.reshape(C, 4 * T), "t_state": state_mask.reshape(C, T),
        "t_carry": carry.reshape(C, T), "t_causal": causal, "t_head": head_of,
        "t_router": router.reshape(P, 8 * P), "t_ident": np.eye(P),
    }
    return {k: np.ascontiguousarray(v, dtype=np.float32) for k, v in out.items()}


def wait(engine, semaphore, value):
    if not isinstance(value, int) or value > 0:
        engine.wait_ge(semaphore, value)


class Shared:
    pass


def build(nc, x, w_up, w_down, w_gate, vecs, t_rope, t_state, t_carry, t_causal, t_head,
          t_router, t_ident, out):
    rows = x.shape[0]
    NB = rows // T
    NT = rows // P
    with ExitStack() as ctx:
        def sb(name, shape, dt=F32):
            return ctx.enter_context(nc.sbuf_tensor(name, shape, dt))

        def sem(name):
            return ctx.enter_context(nc.semaphore(name))

        up = [sb("up_hi", [P, N_UP * P], F32R), sb("up_lo", [P, N_UP * P], F32R)]
        down = sb("down", [P, N_DOWN * P])
        gate_w = sb("gate_w", [P, EXPERTS])
        vec = sb("vec", [P, 5])
        rope = sb("rope", [P, 4, T])
        state_mask = sb("state_mask", [P, T])
        carry = sb("carry", [P, T])
        causal = sb("causal", [P, CHUNK])
        head_of = sb("head_of", [P, 4])
        router = sb("router", [P, 8 * P], F32R)
        ident = sb("ident", [P, P])
        eps = sb("eps", [P, 1])
        xn_all = sb("xn_all", [P, rows])
        y_all = sb("y_all", [P, rows])
        skip_all = sb("skip_all", [P, rows])
        logits = sb("logits", [P, NT * EXPERTS])
        y_var = sb("y_var", [P, NT * HEADS])
        row_mean = sb("row_mean", [P, NT])
        row_rstd = sb("row_rstd", [P, NT])
        row_rms = sb("row_rms", [P, NT])
        SCRATCH = 22 * T
        scratch = sb("scratch", [P, SCRATCH])
        work_r = sb("work_r", [P, 3, T], F32R)
        vexp = sb("vexp", [P, CHUNKS * P])

        def part(i, n=1):
            return scratch[:, i * T:(i + n) * T]

        banks = ctx.enter_context(nc.psum_tensor("banks", [P, 8, T], F32))

        x_rows = x.rearrange("(n p) c -> p n c", p=P)
        out_rows = out.rearrange("(n p) c -> p n c", p=P)
        seqs = xn_all[:, :].rearrange("p (n c) -> p n c", c=P)
        XPARTS = 4

        s_x = [sem(f"x_loaded{i}") for i in range(XPARTS)]
        s_up_raw, s_weights, s_tables = sem("up_loaded"), sem("weights_loaded"), sem("tables_loaded")
        s_rt, s_rope = sem("router_loaded"), sem("rope_loaded")
        s_eps = sem("eps_set")
        s_bn = sem("bn_done")
        s_dchain = sem("vector_step")
        s_var = sem("variances_ready")
        s_std = sem("deviations_ready")
        s_stats = sem("stats_ready")
        s_fold = sem("weights_folded")
        s_up_split = sem("up_split")
        s_zero = sem("pads_zeroed")

        up_raw = skip_all[:, 0:N_UP * P]

        bn = scratch[:, 0:NT * 6]
        small = scratch[:, NT * 6:NT * 6 + 8 * NT]
        two_var = small[:, 0:2 * NT]
        two_std = small[:, 2 * NT:4 * NT]

        with nc.Block() as block:
            @block.sync
            def _(sp):
                n = NT // XPARTS
                for i in range(XPARTS):
                    sp.dma_start(seqs[:, i * n:(i + 1) * n, :], x_rows[:, i * n:(i + 1) * n, :]).then_inc(s_x[i], 16)
                sp.dma_start(down[:], w_down).then_inc(s_weights, 16)
                sp.dma_start(gate_w[:], w_gate).then_inc(s_weights, 16)

            @block.scalar
            def _(act):
                act.dma_start(vec[:], vecs).then_inc(s_up_raw, 16)
                act.dma_start(up_raw, w_up).then_inc(s_up_raw, 16)
                act.dma_start(rope[:, :, :], t_rope.rearrange("p (n t) -> p n t", n=4)).then_inc(s_rope, 16)
                act.wait_ge(s_eps, 1)
                act.wait_ge(s_var, 2)
                nc.scalar.activation(two_std, two_var, ACT.Sqrt).then_inc(s_std, 1)
                act.wait_ge(s_fold, 1)
                nc.scalar.copy(up[0][:, :], up_raw).then_inc(s_up_split, 1)

            @block.gpsimd
            def _(pool):
                pool.dma_start(state_mask[:], t_state).then_inc(s_tables, 16)
                pool.dma_start(carry[:], t_carry).then_inc(s_tables, 16)
                pool.dma_start(causal[:], t_causal).then_inc(s_tables, 16)
                pool.dma_start(head_of[:], t_head).then_inc(s_tables, 16)
                pool.dma_start(ident[:], t_ident).then_inc(s_tables, 16)
                pool.dma_start(y_all[:, 0:8 * P], t_router).then_inc(s_rt, 16)
                nc.gpsimd.memset(vexp[:, :], 0.0).then_inc(s_zero, 1)

            @block.vector
            def _(dve):
                nc.vector.memset(eps[:, :], GN_EPS).then_inc(s_eps, 1)
                dve.wait_ge(s_up_raw, 32)
                nc.vector.tensor_scalar(up_raw[:, 0:RMS_BLOCKS * P], up_raw[:, 0:RMS_BLOCKS * P], vec[:, 0:1], None,
                                        ALU.mult).then_inc(s_dchain, 1)
                v_w = up_raw[:, V * P:(V + 1) * P].rearrange("p (h d) -> p h d", d=HD)
                v_mean = small[:, 7 * NT:7 * NT + HEADS]
                dve.wait_ge(s_dchain, 1)
                nc.vector.tensor_reduce(v_mean, v_w, AX, ALU.add).then_inc(s_dchain, 1)
                dve.wait_ge(s_dchain, 2)
                nc.vector.tensor_scalar(v_mean, v_mean, 1.0 / HD, None, ALU.mult).then_inc(s_dchain, 1)
                dve.wait_ge(s_dchain, 3)
                nc.vector.tensor_tensor(v_w, v_w, v_mean.unsqueeze(2).broadcast_to([P, HEADS, HD]),
                                        ALU.subtract).then_inc(s_fold, 1)
                per = NT // XPARTS
                for i in range(XPARTS):
                    dve.wait_ge(s_x[i], 16)
                    with dve.Fori(i * per // 4, (i + 1) * per // 4) as n:
                        for j in range(4):
                            nc.vector.bn_stats(bn[:, bass.ds(n * 24 + j * 6, 6)],
                                               xn_all[:, bass.ds(n * T + j * P, P)]).then_inc(s_bn, 1)
                dve.wait_ge(s_bn, NT)
                b = bn.rearrange("p (n s) -> p n s", s=6)
                mean_sum, mean_gap = small[:, 4 * NT:5 * NT], small[:, 5 * NT:6 * NT]
                var, var_eps = two_var[:, NT:2 * NT], two_var[:, 0:NT]
                nc.vector.tensor_tensor(mean_sum, b[:, :, 1], b[:, :, 4], ALU.add).then_inc(s_dchain, 1)
                nc.vector.tensor_tensor(mean_gap, b[:, :, 1], b[:, :, 4], ALU.subtract).then_inc(s_dchain, 1)
                nc.vector.tensor_tensor(var_eps, b[:, :, 2], b[:, :, 5], ALU.add).then_inc(s_dchain, 1)
                dve.wait_ge(s_dchain, 6)
                nc.vector.tensor_scalar(row_mean[:, :], mean_sum, 0.5, None, ALU.mult).then_inc(s_dchain, 1)
                nc.vector.scalar_tensor_tensor(mean_gap, mean_gap, 0.25, mean_gap, ALU.mult, ALU.mult).then_inc(s_dchain, 1)
                dve.wait_ge(s_dchain, 8)
                nc.vector.scalar_tensor_tensor(var, var_eps, 1.0 / P, mean_gap, ALU.mult, ALU.add).then_inc(s_var, 1)
                dve.wait_ge(s_var, 1)
                nc.vector.tensor_scalar(var_eps, var, LN_EPS, None, ALU.add).then_inc(s_var, 1)
                dve.wait_ge(s_up_split, 1)
                nc.vector.tensor_tensor(up[1][:, :], up_raw, up[0][:, :].bitcast(F32), ALU.subtract).then_inc(s_up_split, 1)
                dve.wait_ge(s_rt, 16)
                nc.vector.tensor_copy(router[:, :], y_all[:, 0:8 * P]).then_inc(s_up_split, 1)
                dve.wait_ge(s_std, 1)
                nc.vector.reciprocal(row_rstd[:, :], two_std[:, 0:NT]).then_inc(s_dchain, 1)
                dve.wait_ge(s_dchain, 9)
                nrm = small[:, 6 * NT:7 * NT]
                nc.vector.tensor_tensor(nrm, two_std[:, NT:2 * NT], row_rstd[:, :], ALU.mult).then_inc(s_dchain, 1)
                dve.wait_ge(s_dchain, 10)
                nc.vector.tensor_scalar(nrm, nrm, 1e-8, None, ALU.max).then_inc(s_dchain, 1)
                dve.wait_ge(s_dchain, 11)
                nc.vector.reciprocal(mean_sum, nrm).then_inc(s_dchain, 1)
                dve.wait_ge(s_dchain, 12)
                nc.vector.tensor_tensor(row_rms[:, :], mean_sum, row_rstd[:, :], ALU.mult).then_inc(s_stats, 1)
                dve.wait_ge(s_stats, 1)

        g = Shared()
        g.NB, g.NT, g.banks, g.part, g.work_r = NB, NT, banks, part, work_r
        g.up, g.down, g.gate_w, g.router, g.vec, g.eps = up, down, gate_w, router, vec, eps
        g.rope, g.state_mask, g.carry, g.causal, g.head_of, g.ident = rope, state_mask, carry, causal, head_of, ident
        g.xn_all, g.y_all, g.skip_all, g.logits, g.y_var, g.vexp = xn_all, y_all, skip_all, logits, y_var, vexp
        g.row_mean, g.row_rstd, g.row_rms = row_mean, row_rstd, row_rms
        g.x_rows, g.out_rows = x_rows, out_rows
        g.s_up_split, g.s_weights, g.s_tables, g.s_rope, g.s_zero = s_up_split, s_weights, s_tables, s_rope, s_zero
        attend(nc, sem, g)
        route(nc, sem, g)
        combine(nc, sem, g)


def attend(nc, sem, g):
    NB, banks, part, up, down = g.NB, g.banks, g.part, g.up, g.down
    xn_all, y_all, skip_all, logits, y_var = g.xn_all, g.y_all, g.skip_all, g.logits, g.y_var
    ident, rope, vec, vexp = g.ident, g.rope, g.vec, g.vexp
    xn, xs, xn_t = part(0), part(1), part(2)
    ff = part(3, 2)
    cosine, sine = part(5), part(6)
    q_t, k_t = part(7), part(8)
    k_heads = part(9, 4)
    k_rows, v_rows = part(13), part(14)
    probs = part(15, 4)
    u_in, states = part(19), part(20)
    y_sq = part(21)
    xs_t = [g.work_r[:, 0, :], g.work_r[:, 1, :]]

    s_norm = sem("a_rows_normed")
    s_tr = sem("a_transposed")
    s_xnt = sem("a_xn_t_ready")
    s_xst = sem("a_xs_t_ready")
    s_keep = sem("a_xn_t_kept")
    s_gate = sem("a_logits_ready")
    s_gatek = sem("a_logits_kept")
    s_ffup = sem("a_ff_up_done")
    s_gelu = sem("a_gelu_ready")
    s_ffdn = sem("a_ff_down_done")
    s_skip = sem("a_skip_kept")
    s_kp = sem("a_k_projected")
    s_kr = sem("a_k_rotated")
    s_kt = sem("a_k_t_ready")
    s_kh = sem("a_k_heads_ready")
    s_qp = sem("a_q_projected")
    s_qr = sem("a_q_rotated")
    s_qt = sem("a_q_t_ready")
    s_vp = sem("a_v_projected")
    s_vr = sem("a_v_rows_ready")
    s_vx = sem("a_v_expanded")
    s_ktr = sem("a_k_transposed")
    s_krow = sem("a_k_rows_ready")
    s_u = sem("a_updates_done")
    s_um = sem("a_updates_masked")
    s_st = sem("a_states_ready")
    s_sc = sem("a_scores_done")
    s_p = sem("a_probs_ready")
    s_y = sem("a_y_done")
    s_yk = sem("a_y_kept")
    s_yv = sem("a_y_variances")
    s_up_split, s_weights, s_tables, s_zero = g.s_up_split, g.s_weights, g.s_tables, g.s_zero

    def split_matmul(out, block, rhs, start=True):
        for i, (a, c) in enumerate(PARTS):
            last = nc.tensor.matmul(out, up[a][:, block * P:(block + 1) * P], rhs[c],
                                    start=start and i == 0, stop=i == 2)
        return last

    with nc.Block() as block:
        @block.sync
        def _(sp):
            with sp.Fori(0, NB) as b:
                wait(sp, s_xnt, b + 1)
                wait(sp, s_norm, b + 1)
                sp.dma_start(xn_all[:, bass.ds(b * T, T)], xn_t).then_inc(s_keep, 16)
            sp.wait_ge(s_keep, 16 * NB)

        @block.tensor
        def _(pe):
            pe.wait_ge(s_up_split, 3)
            pe.wait_ge(s_weights, 32)
            pe.wait_ge(s_tables, 80)

            def transposes(b):
                wait(pe, s_norm, b + 1)
                wait(pe, s_vr, b)
                wait(pe, s_krow, b)
                for j in range(TILES):
                    nc.tensor.transpose(banks[:, 4, j * P:(j + 1) * P], xn[:, j * P:(j + 1) * P], ident[:, :])
                for j in range(TILES):
                    last = nc.tensor.transpose(banks[:, 5, j * P:(j + 1) * P], xs[:, j * P:(j + 1) * P], ident[:, :])
                last.then_inc(s_tr, 1)

            def feed_forward_up(b):
                wait(pe, s_xst, 2 * b + 2)
                wait(pe, s_skip, b)
                wait(pe, s_gatek, b)
                for k in range(2):
                    split_matmul(banks[:, 6 + k, :], FF + k, xs_t).then_inc(s_ffup, 1)

            def project_k(b):
                wait(pe, s_xnt, b + 1)
                split_matmul(banks[:, 4, :], K, xs_t)
                split_matmul(banks[:, 5, :], KS, xs_t).then_inc(s_kp, 1)

            def feed_forward_down(b):
                wait(pe, s_gelu, 2 * b + 2)
                for k in range(2):
                    last = nc.tensor.matmul(banks[:, 6, :], down[:, (D_FF + k) * P:(D_FF + k + 1) * P],
                                            ff[:, k * T:(k + 1) * T], start=k == 0, stop=k == 1)
                last.then_inc(s_ffdn, 1)

            def gate(b):
                for j in range(TILES):
                    last = nc.tensor.matmul(banks[:, 7, j * EXPERTS:(j + 1) * EXPERTS], xn_t[:, j * P:(j + 1) * P],
                                            g.gate_w[:, :], start=True, stop=True)
                last.then_inc(s_gate, 1)

            def project_q(b):
                wait(pe, s_kr, 2 * b + 2)
                split_matmul(banks[:, 4, :], Q, xs_t)
                split_matmul(banks[:, 5, :], QS, xs_t).then_inc(s_qp, 1)

            def project_v(b):
                wait(pe, s_qr, 2 * b + 2)
                for j in range(TILES):
                    for i, (a, c) in enumerate(PARTS):
                        last = nc.tensor.matmul(banks[:, 4, j * P:(j + 1) * P], xs_t[a][:, j * P:(j + 1) * P],
                                                up[c][:, V * P:(V + 1) * P], start=i == 0, stop=i == 2)
                last.then_inc(s_vp, 1)

            def k_by_rows(b):
                wait(pe, s_kt, b + 1)
                for j in range(TILES):
                    last = nc.tensor.transpose(banks[:, 5, j * P:(j + 1) * P], k_t[:, j * P:(j + 1) * P], ident[:, :])
                last.then_inc(s_ktr, 1)

            def wait_for_state_updates(b):
                wait(pe, s_krow, b + 1)
                wait(pe, s_vr, b + 1)
                wait(pe, s_yk, 2 * b)

            def state_updates(b):
                for j in range(TILES):
                    for c in range(4):
                        for h in range(GROUPS):
                            rows = slice(32 * c, 32 * c + 32)
                            cols = slice(j * P + 32 * h, j * P + 32 * h + 32)
                            last = nc.tensor.matmul(banks[32 * h:32 * h + 32, c, 32 * j:32 * j + 32],
                                                    k_rows[rows, cols], v_rows[rows, cols], start=True, stop=True)
                last.then_inc(s_u, 1)

            def scores(b):
                wait(pe, s_kh, b + 1)
                wait(pe, s_qt, b + 1)
                wait(pe, s_um, b + 1)
                for n in range(CHUNKS):
                    for h in range(GROUPS):
                        rows, cols = slice(32 * h, 32 * h + 32), slice(CHUNK * n, CHUNK * n + CHUNK)
                        last = nc.tensor.matmul(banks[:, h, cols], k_heads[rows, n * P:(n + 1) * P], q_t[rows, cols],
                                                start=True, stop=True)
                last.then_inc(s_sc, 1)

            def outputs(b):
                wait(pe, s_st, b + 1)
                wait(pe, s_vx, b + 1)
                wait(pe, s_p, 4 * b + 4)
                pr = probs.rearrange("p (h t) -> p h t", h=GROUPS)
                for n in range(CHUNKS):
                    j, c = n // 4, n % 4
                    for h in range(GROUPS):
                        nc.tensor.matmul(banks[32 * c:32 * c + 32, h, 32 * j:32 * j + 32],
                                         pr[:, h, CHUNK * n:CHUNK * n + CHUNK],
                                         vexp[:, n * P + 32 * h:n * P + 32 * h + 32],
                                         start=j == 0, stop=n == 0, skip_group_check=True)
                st = states.rearrange("p (e n) -> p e n", n=CHUNKS)
                for n in range(1, CHUNKS):
                    j, c = n // 4, n % 4
                    for h in range(GROUPS):
                        rows = slice(32 * h, 32 * h + 32)
                        last = nc.tensor.matmul(banks[32 * c:32 * c + 32, h, 32 * j:32 * j + 32],
                                                q_t[rows, CHUNK * n:CHUNK * n + CHUNK], st[rows, :, n - 1],
                                                start=False, stop=True, skip_group_check=True)
                last.then_inc(s_y, 1)

            def front_before_outputs(b):
                feed_forward_up(b)
                project_k(b)
                feed_forward_down(b)
                gate(b)

            def front_after_outputs(b):
                project_q(b)
                project_v(b)
                k_by_rows(b)

            transposes(0)
            front_before_outputs(0)
            front_after_outputs(0)

            def body(b):
                wait_for_state_updates(b)
                transposes(b + 1)
                state_updates(b)
                scores(b)
                front_before_outputs(b + 1)
                outputs(b)
                front_after_outputs(b + 1)

            body(0)
            with pe.Fori(1, NB - 1) as b:
                body(b)
            wait_for_state_updates(NB - 1)
            state_updates(NB - 1)
            scores(NB - 1)
            outputs(NB - 1)

        @block.scalar
        def _(act):
            vx = vexp[:, :].rearrange("p (j c g h e) -> p j c g h e", j=TILES, c=4, g=GROUPS, h=4)
            vr = v_rows.rearrange("p (j g h e) -> p j g h e", j=TILES, g=GROUPS, h=4)

            def x_by_channels(b):
                wait(act, s_tr, b + 1)
                wait(act, s_keep, b * 16)
                wait(act, s_gate, b)
                wait(act, s_skip, b)
                wait(act, s_vp, b)
                nc.scalar.copy(xs_t[0], banks[:, 5, :]).then_inc(s_xst, 1)
                nc.scalar.copy(xn_t, banks[:, 4, :]).then_inc(s_xnt, 1)

            def gelu(b):
                wait(act, s_ffdn, b)
                for k in range(2):
                    wait(act, s_ffup, 2 * b + k + 1)
                    nc.scalar.activation(ff[:, k * T:(k + 1) * T], banks[:, 6 + k, :], ACT.Gelu).then_inc(s_gelu, 1)

            def keep_logits(b):
                wait(act, s_gate, b + 1)
                nc.scalar.copy(logits[:, bass.ds(b * (TILES * EXPERTS), TILES * EXPERTS)],
                               banks[:, 7, 0:TILES * EXPERTS]).then_inc(s_gatek, 1)

            def rows_of_v_and_k(b):
                wait(act, s_vp, b + 1)
                wait(act, s_u, b)
                nc.scalar.copy(v_rows, banks[:, 4, :]).then_inc(s_vr, 1)
                wait(act, s_ktr, b + 1)
                nc.scalar.copy(k_rows, banks[:, 5, :]).then_inc(s_krow, 1)

            def expand_v(b):
                wait(act, s_vr, b + 1)
                wait(act, s_y, b)
                for h in range(4):
                    for c in range(4):
                        last = nc.scalar.copy(vx[32 * h:32 * h + 32, :, c, :, h, :], vr[32 * c:32 * c + 32, :, :, h, :])
                last.then_inc(s_vx, 1)

            def keep_y(b):
                wait(act, s_y, b + 1)
                y_b = banks[:, 0:4, 0:P].rearrange("p g (j e) -> p j g e", j=TILES)
                nc.scalar.copy(y_all[:, bass.ds(b * T, T)].rearrange("p (j g e) -> p j g e", j=TILES, g=GROUPS),
                               y_b).then_inc(s_yk, 1)
                wait(act, s_yv, b)
                nc.scalar.activation(y_sq.rearrange("p (j g e) -> p j g e", j=TILES, g=GROUPS),
                                     y_b, ACT.Square).then_inc(s_yk, 1)

            act.wait_ge(s_zero, 1)
            x_by_channels(0)
            gelu(0)
            keep_logits(0)
            rows_of_v_and_k(0)

            def body(b):
                expand_v(b)
                x_by_channels(b + 1)
                gelu(b + 1)
                keep_logits(b + 1)
                keep_y(b)
                rows_of_v_and_k(b + 1)

            body(0)
            with act.Fori(1, NB - 1) as b:
                body(b)
            expand_v(NB - 1)
            keep_y(NB - 1)

        @block.vector
        def _(dve):
            row_mean, row_rstd, row_rms = g.row_mean, g.row_rstd, g.row_rms

            def norm_rows(b):
                wait(dve, s_tr, b)
                for j in range(TILES):
                    tile = xn_all[:, bass.ds(b * T + j * P, P)]
                    mean = row_mean[:, bass.ds(b * TILES + j, 1)]
                    nc.vector.tensor_scalar(xn[:, j * P:(j + 1) * P], tile, mean,
                                            row_rstd[:, bass.ds(b * TILES + j, 1)], ALU.subtract, ALU.mult)
                    last = nc.vector.tensor_scalar(xs[:, j * P:(j + 1) * P], tile, mean,
                                                   row_rms[:, bass.ds(b * TILES + j, 1)], ALU.subtract, ALU.mult)
                last.then_inc(s_norm, 1)

            def split_x(b):
                wait(dve, s_xst, 2 * b + 1)
                nc.vector.tensor_tensor(xs_t[1], banks[:, 5, :], xs_t[0].bitcast(F32), ALU.subtract).then_inc(s_xst, 1)

            def rotate(b, s_projected, s_rotated, at):
                wait(dve, s_projected, b + 1)
                if at == 0:
                    wait(dve, s_kt, b + 1)
                else:
                    wait(dve, s_qt, b)
                nc.vector.tensor_tensor(cosine, banks[:, 4, :], rope[:, at, :], ALU.mult).then_inc(s_rotated, 1)
                nc.vector.tensor_tensor(sine, banks[:, 5, :], rope[:, at + 1, :], ALU.mult).then_inc(s_rotated, 1)

            def keep_skip(b):
                wait(dve, s_ffdn, b + 1)
                wait(dve, s_xnt, b + 1)
                nc.vector.scalar_tensor_tensor(skip_all[:, bass.ds(b * T, T)], banks[:, 6, :], vec[:, 4:5], xn_t,
                                               ALU.add, ALU.add).then_inc(s_skip, 1)

            def carry_states(b):
                wait(dve, s_u, b + 1)
                wait(dve, s_st, b)
                nc.vector.tensor_tensor(u_in.rearrange("p (e j c) -> p j c e", e=32, j=TILES),
                                        banks[:, 0:4, 0:P].rearrange("p c (j e) -> p j c e", j=TILES),
                                        g.state_mask[:, :].rearrange("p (e j c) -> p j c e", e=32, j=TILES),
                                        ALU.mult).then_inc(s_um, 1)
                wait(dve, s_um, b + 1)
                wait(dve, s_y, b)
                nc.vector.tensor_tensor_scan(states, g.carry[:, :], u_in, 0.0, ALU.mult, ALU.add).then_inc(s_st, 1)

            def mask_scores(b):
                wait(dve, s_sc, b + 1)
                wait(dve, s_y, b)
                for h in range(GROUPS):
                    nc.vector.tensor_tensor(probs[:, h * T:(h + 1) * T].rearrange("p (n t) -> p n t", t=CHUNK),
                                            banks[:, h, :].rearrange("p (n t) -> p n t", t=CHUNK),
                                            g.causal[:, :].unsqueeze(1).broadcast_to([P, CHUNKS, CHUNK]),
                                            ALU.mult).then_inc(s_p, 1)

            def variances(b):
                wait(dve, s_yk, 2 * b + 2)
                nc.vector.tensor_reduce(y_var[:, bass.ds(b * (TILES * HEADS), TILES * HEADS)],
                                        y_sq.rearrange("p (h e) -> p h e", e=HD), AX, ALU.add).then_inc(s_yv, 1)

            norm_rows(0)
            split_x(0)
            dve.wait_ge(s_tables, 80)
            dve.wait_ge(g.s_rope, 16)
            rotate(0, s_kp, s_kr, 2)
            keep_skip(0)
            rotate(0, s_qp, s_qr, 0)
            norm_rows(1)

            def body(b):
                carry_states(b)
                split_x(b + 1)
                mask_scores(b)
                rotate(b + 1, s_kp, s_kr, 2)
                keep_skip(b + 1)
                variances(b)
                rotate(b + 1, s_qp, s_qr, 0)

            body(0)
            norm_rows(2)
            with dve.Fori(1, NB - 2) as b:
                body(b)
                norm_rows(b + 2)
            body(NB - 2)
            carry_states(NB - 1)
            mask_scores(NB - 1)
            variances(NB - 1)

        @block.gpsimd
        def _(pool):
            def sum_k(b):
                wait(pool, s_kr, 2 * b + 2)
                wait(pool, s_ktr, b)
                wait(pool, s_kh, b)
                nc.gpsimd.tensor_tensor(k_t, cosine, sine, ALU.add).then_inc(s_kt, 1)
                wait(pool, s_kt, b + 1)
                wait(pool, s_sc, b)
                heads = k_heads.rearrange("p (n h s) -> p n h s", h=4, s=CHUNK)
                k_chunks = k_t.rearrange("p (n s) -> p n s", s=CHUNK)
                nc.gpsimd.tensor_tensor(heads[:, :, 0, :], k_chunks,
                                        g.head_of[:, 0:1].unsqueeze(2).broadcast_to([P, CHUNKS, CHUNK]), ALU.mult)
                for h in range(1, 4):
                    last = nc.gpsimd.tensor_scalar(heads[:, :, h, :], k_chunks, g.head_of[:, h:h + 1], None, ALU.mult)
                last.then_inc(s_kh, 1)

            def sum_q(b):
                wait(pool, s_qr, 2 * b + 2)
                wait(pool, s_y, b)
                nc.gpsimd.tensor_tensor(q_t, cosine, sine, ALU.add).then_inc(s_qt, 1)

            pool.wait_ge(s_tables, 80)
            sum_k(0)
            sum_q(0)
            with pool.Fori(1, NB) as b:
                sum_k(b)
                sum_q(b)


def route(nc, sem, g):
    NT, part = g.NT, g.part
    logits, y_var, eps = g.logits, g.y_var, g.eps
    n = NT * EXPERTS
    score, kept, rank, less, chosen = part(0, 2), part(2, 2), part(4, 2), part(6, 2), part(8, 2)
    top = part(10, 2)
    g.comb_all = logits
    g.y_rstd = y_var
    s_sig = sem("r_scores_ready")
    s_ystd = sem("r_y_deviations")
    s_step = sem("r_step")
    s_done = sem("r_done")
    G4 = NT * N_GROUP

    with nc.Block() as block:
        @block.scalar
        def _(act):
            nc.scalar.activation(score, logits[:, :], ACT.Sigmoid).then_inc(s_sig, 1)
            nc.scalar.activation(chosen, y_var[:, :], ACT.Sqrt, bias=eps[:, 0:1], scale=1.0 / HD).then_inc(s_ystd, 1)

        @block.vector
        def _(dve):
            steps = [0]

            def step(instruction):
                instruction.then_inc(s_step, 1)
                steps[0] += 1
                dve.wait_ge(s_step, steps[0])

            dve.wait_ge(s_ystd, 1)
            step(nc.vector.reciprocal(y_var[:, :], chosen))
            dve.wait_ge(s_sig, 1)
            s4 = score.rearrange("p (g e) -> p g e", e=4)
            a, b, c, d = (s4[:, :, i] for i in range(4))
            f = [top[:, i * G4:(i + 1) * G4] for i in range(4)]
            nc.vector.tensor_tensor(f[0], a, b, ALU.max)
            nc.vector.tensor_tensor(f[1], a, b, ALU.min)
            nc.vector.tensor_tensor(f[2], c, d, ALU.max)
            step(nc.vector.tensor_tensor(f[3], c, d, ALU.min))
            step(nc.vector.tensor_tensor(f[1], f[1], f[3], ALU.max))
            step(nc.vector.tensor_tensor(f[3], f[0], f[2], ALU.min))
            step(nc.vector.tensor_tensor(f[1], f[1], f[3], ALU.max))
            step(nc.vector.tensor_tensor(f[0], f[0], f[2], ALU.max))
            step(nc.vector.tensor_tensor(f[0], f[0], f[1], ALU.add))
            gs = f[0].rearrange("p (t g) -> p t g", g=N_GROUP)
            lost = f[1].rearrange("p (t g) -> p t g", g=N_GROUP)
            win = f[2].rearrange("p (t g) -> p t g", g=N_GROUP)

            def rank_all(values, ranks, wins, width):
                step(nc.vector.memset(ranks, 0.0))
                for off in range(1, width):
                    lo, hi = slice(0, width - off), slice(off, width)
                    step(nc.vector.tensor_tensor(wins[:, :, lo], values[:, :, lo], values[:, :, hi], ALU.is_ge))
                    step(nc.vector.tensor_tensor(ranks[:, :, hi], ranks[:, :, hi], wins[:, :, lo], ALU.add))
                    step(nc.vector.scalar_tensor_tensor(ranks[:, :, lo], ranks[:, :, lo], 1.0, wins[:, :, lo],
                                                        ALU.add, ALU.subtract))

            rank_all(gs, lost, win, N_GROUP)
            step(nc.vector.tensor_scalar(f[3], f[1], float(TOPK_GROUP) - 0.5, None, ALU.is_lt))
            step(nc.vector.tensor_tensor(kept.rearrange("p (g e) -> p g e", e=4), s4,
                                         f[3].unsqueeze(2).broadcast_to([P, G4, 4]), ALU.mult))
            k3 = kept.rearrange("p (t e) -> p t e", e=EXPERTS)
            r3 = rank.rearrange("p (t e) -> p t e", e=EXPERTS)
            l3 = less.rearrange("p (t e) -> p t e", e=EXPERTS)
            rank_all(k3, r3, l3, EXPERTS)
            step(nc.vector.scalar_tensor_tensor(chosen, rank, float(TOP_K) - 0.5, score, ALU.is_lt, ALU.mult))
            total, inverse = top[:, 0:NT], top[:, NT:2 * NT]
            step(nc.vector.tensor_reduce(total, chosen.rearrange("p (t e) -> p t e", e=EXPERTS), AX, ALU.add))
            step(nc.vector.tensor_scalar(total, total, 1e-20, None, ALU.add))
            step(nc.vector.reciprocal(inverse, total))
            step(nc.vector.tensor_scalar(inverse, inverse, ROUTED_SCALING, None, ALU.mult))
            nc.vector.tensor_tensor(logits[:, :].rearrange("p (t e) -> p t e", e=EXPERTS),
                                    chosen.rearrange("p (t e) -> p t e", e=EXPERTS),
                                    inverse.unsqueeze(2).broadcast_to([P, NT, EXPERTS]), ALU.mult).then_inc(s_done, 1)
            dve.wait_ge(s_done, 1)


def combine(nc, sem, g):
    NB, banks, part, up, down, router = g.NB, g.banks, g.part, g.up, g.down, g.router
    xn_all, y_all, skip_all = g.xn_all, g.y_all, g.skip_all
    comb_all, y_rstd, vec, ident = g.comb_all, g.y_rstd, g.vec, g.ident
    x_rows, out_rows = g.x_rows, g.out_rows
    x_t = [g.work_r[:, 0, :], g.work_r[:, 1, :]]
    comb_t = g.work_r[:, 2, :]
    yn, y_t, gated, y_gated = part(0), part(1), part(2), part(3)
    total, silu_ffn, product = part(4), part(5), part(6)
    x_in, result = part(7), part(8)
    act_out = [part(9), part(10)]
    hidden = [part(11 + i) for i in range(3)]
    shared = [part(14), part(15)]
    comb_parts = part(16)[:, 0:TILES * 2 * EXPERTS]
    N_MOE, N_SH = 8, 2
    N_BLK = N_MOE + N_SH
    U, B, O, G, YT, CT = 0, 2, 4, 5, 6, 7

    s_zero = sem("c_comb_t_zeroed")
    s_xhi, s_xlo = sem("c_x_hi"), sem("c_x_lo")
    s_cp = sem("c_comb_parts")
    s_ct = sem("c_comb_transposed")
    s_ctr = sem("c_comb_t_ready")
    s_yn = sem("c_y_normed")
    s_ytr = sem("c_y_transposed")
    s_yt = sem("c_y_t_ready")
    s_gp = sem("c_gate_projected")
    s_gs = sem("c_gate_ready")
    s_yg = sem("c_y_gated")
    s_pr = sem("c_y_projected")
    s_tot = sem("c_branch_ready")
    s_up = sem("c_up_done")
    s_silu = sem("c_silu_moe")
    s_sh = sem("c_silu_shared")
    s_bc = sem("c_weights_spread")
    s_h = sem("c_hidden_ready")
    s_dn = sem("c_down_done")
    s_g = sem("c_ffn_silu_ready")
    s_prod = sem("c_product_ready")
    s_bt = sem("c_product_by_rows")
    s_res = sem("c_result_ready")
    s_xin = sem("c_x_loaded")
    s_out = sem("c_out_stored")

    def sequences(engine, body, end=None):
        body(0, True)
        body(1, False)
        with engine.Fori(2, NB) as b:
            body(b, False)
        if end is not None:
            end(NB - 1)

    with nc.Block() as block:
        @block.sync
        def _(sp):
            def body(b, first):
                if not first:
                    wait(sp, s_res, b)
                sp.dma_start(x_in.rearrange("p (j c) -> p j c", c=P), x_rows[:, bass.ds(b * TILES, TILES), :]
                             ).then_inc(s_xin, 16)
            sequences(sp, body)

        @block.gpsimd
        def _(pool):
            def store(b):
                wait(pool, s_res, b + 1)
                pool.dma_start(out_rows[:, bass.ds(b * TILES, TILES), :], result.rearrange("p (j c) -> p j c", c=P)
                               ).then_inc(s_out, 16)

            def body(b, first):
                if not first:
                    store(b - 1)
                wait(pool, s_gs, b + 1)
                wait(pool, s_yt, b + 1)
                if not first:
                    wait(pool, s_pr, b)
                nc.gpsimd.tensor_tensor(y_gated, gated, y_t, ALU.mult).then_inc(s_yg, 1)
            sequences(pool, body, store)
            pool.wait_ge(s_out, 16 * NB)

        @block.tensor
        def _(pe):
            pe.wait_ge(s_zero, 1)

            def split_matmul(out, block, rhs):
                for i, (a, c) in enumerate(PARTS):
                    last = nc.tensor.matmul(out, up[a][:, block * P:(block + 1) * P], rhs[c], start=i == 0, stop=i == 2)
                return last

            def by_rows(b):
                wait(pe, s_prod, b + 1)
                for j in range(TILES):
                    last = nc.tensor.transpose(banks[:, CT, j * P:(j + 1) * P], product[:, j * P:(j + 1) * P], ident[:, :])
                last.then_inc(s_bt, 1)

            def block_up(b, first, k):
                if not (first and k < 2):
                    if k < 2:
                        wait(pe, s_silu, b * N_MOE + k - 1)
                    elif k < 4:
                        wait(pe, s_sh, b * N_SH + k - 1)
                    else:
                        wait(pe, s_silu, b * N_MOE + k - 3)
                split_matmul(banks[:, U + k % 2, :], SHARED + k, x_t).then_inc(s_up, 1)

            def spread(b, first, m):
                if not (first and m < 2):
                    wait(pe, s_h, b * N_MOE + m - 1)
                nc.tensor.matmul(banks[:, B + m % 2, :], router[:, m * P:(m + 1) * P], comb_t,
                                 start=True, stop=True).then_inc(s_bc, 1)

            def block_down(b, k):
                if k < N_SH:
                    wait(pe, s_sh, b * N_SH + k + 1)
                    rhs, at = shared[k], D_SHARED + k
                else:
                    wait(pe, s_h, b * N_MOE + k - 1)
                    rhs, at = hidden[(k - N_SH) % 3], D_MOE + k - N_SH
                nc.tensor.matmul(banks[:, O, :], down[:, at * P:(at + 1) * P], rhs, start=k == 0,
                                 stop=k == N_BLK - 1).then_inc(s_dn, 1)

            def body(b, first):
                wait(pe, s_xhi, b + 1)
                wait(pe, s_xlo, b + 1)
                block_up(b, first, 0)
                block_up(b, first, 1)
                wait(pe, s_cp, 2 * b + 2)
                if not first:
                    wait(pe, s_res, b - 1)
                for j in range(TILES):
                    last = nc.tensor.transpose(banks[0:2 * EXPERTS, CT, j * P:(j + 1) * P],
                                               comb_parts[:, j * 2 * EXPERTS:(j + 1) * 2 * EXPERTS], ident[:, :])
                last.then_inc(s_ct, 1)
                if not first:
                    wait(pe, s_tot, b)
                split_matmul(banks[:, G, :], GATED, x_t).then_inc(s_gp, 1)
                block_up(b, first, 2)
                if not first:
                    wait(pe, s_g, b)
                block_down(b, 0)
                wait(pe, s_ctr, b + 1)
                if not first:
                    by_rows(b - 1)
                spread(b, first, 0)
                wait(pe, s_yn, b + 1)
                if not first:
                    wait(pe, s_yt, b)
                for j in range(TILES):
                    last = nc.tensor.transpose(banks[:, YT, j * P:(j + 1) * P], yn[:, j * P:(j + 1) * P], ident[:, :])
                last.then_inc(s_ytr, 1)
                block_up(b, first, 3)
                block_down(b, 1)
                spread(b, first, 1)
                for k in range(4, N_BLK):
                    block_up(b, first, k)
                    block_down(b, k - 2)
                    spread(b, first, k - 2)
                    if k == 7:
                        wait(pe, s_yg, b + 1)
                        nc.tensor.matmul(banks[:, G, :], down[:, D_PROJ * P:(D_PROJ + 1) * P], y_gated,
                                         start=True, stop=True).then_inc(s_pr, 1)
                block_down(b, N_BLK - 2)
                block_down(b, N_BLK - 1)

            sequences(pe, body, by_rows)

        @block.scalar
        def _(act):
            def block_silu(b, first, k):
                wait(act, s_up, b * N_BLK + k + 1)
                if k < N_SH:
                    if not first:
                        wait(act, s_dn, b * N_BLK + k + 1 - N_BLK)
                    nc.scalar.activation(shared[k], banks[:, U + k % 2, :], ACT.Silu).then_inc(s_sh, 1)
                else:
                    m = k - N_SH
                    if not (first and m < 2):
                        wait(act, s_h, b * N_MOE + m - 1)
                    nc.scalar.activation(act_out[m % 2], banks[:, U + k % 2, :], ACT.Silu).then_inc(s_silu, 1)

            def silu_of_sum(b):
                wait(act, s_dn, b * N_BLK + N_BLK)
                wait(act, s_prod, b)
                nc.scalar.activation(silu_ffn, banks[:, O, :], ACT.Silu).then_inc(s_g, 1)

            def body(b, first):
                wait(act, s_up, b * N_BLK)
                wait(act, s_gp, b)
                nc.scalar.copy(x_t[0], xn_all[:, bass.ds(b * T, T)]).then_inc(s_xhi, 1)
                if not first:
                    silu_of_sum(b - 1)
                block_silu(b, first, 0)
                block_silu(b, first, 1)
                wait(act, s_ct, b + 1)
                wait(act, s_bc, b * N_MOE)
                nc.scalar.copy(comb_t[0:2 * EXPERTS, :], banks[0:2 * EXPERTS, CT, :]).then_inc(s_ctr, 1)
                wait(act, s_gp, b + 1)
                wait(act, s_yg, b)
                nc.scalar.activation(gated, banks[:, G, :], ACT.Silu, bias=vec[:, 3:4]).then_inc(s_gs, 1)
                block_silu(b, first, 2)
                wait(act, s_ytr, b + 1)
                nc.scalar.activation(y_t, banks[:, YT, :], ACT.Identity, bias=vec[:, 2:3], scale=vec[:, 1:2]).then_inc(s_yt, 1)
                for k in range(3, N_BLK):
                    block_silu(b, first, k)

            sequences(act, body, silu_of_sum)

        @block.vector
        def _(dve):
            nc.vector.memset(comb_t.bitcast(F32), 0.0).then_inc(s_zero, 1)
            comb_halves = comb_parts.rearrange("p (j w e) -> p j w e", j=TILES, w=2)

            def multiply(b):
                wait(dve, s_g, b + 1)
                wait(dve, s_tot, b + 1)
                wait(dve, s_bt, b)
                nc.vector.tensor_tensor(product, total, silu_ffn, ALU.mult).then_inc(s_prod, 1)

            def residual(b):
                wait(dve, s_bt, b + 1)
                wait(dve, s_xin, b * 16 + 16)
                wait(dve, s_out, b * 16)
                nc.vector.tensor_tensor(result, banks[:, CT, :], x_in, ALU.add).then_inc(s_res, 1)

            def body(b, first):
                wait(dve, s_xhi, b + 1)
                nc.vector.tensor_tensor(x_t[1], xn_all[:, bass.ds(b * T, T)], x_t[0].bitcast(F32),
                                        ALU.subtract).then_inc(s_xlo, 1)
                comb = comb_all[:, bass.ds(b * (TILES * EXPERTS), TILES * EXPERTS)].rearrange("p (j e) -> p j e", j=TILES)
                wait(dve, s_ct, b)
                nc.vector.tensor_copy(comb_halves[:, :, 0, :].bitcast(F32R), comb).then_inc(s_cp, 1)
                wait(dve, s_cp, 2 * b + 1)
                nc.vector.tensor_tensor(comb_halves[:, :, 1, :].bitcast(F32R), comb, comb_halves[:, :, 0, :],
                                        ALU.subtract).then_inc(s_cp, 1)
                wait(dve, s_ytr, b)
                nc.vector.tensor_tensor(yn.rearrange("p (h e) -> p h e", e=HD),
                                        y_all[:, bass.ds(b * T, T)].rearrange("p (h e) -> p h e", e=HD),
                                        y_rstd[:, bass.ds(b * (TILES * HEADS), TILES * HEADS)].unsqueeze(2).broadcast_to(
                                            [P, TILES * HEADS, HD]), ALU.mult).then_inc(s_yn, 1)
                if not first:
                    multiply(b - 1)
                for m in range(N_MOE):
                    wait(dve, s_silu, b * N_MOE + m + 1)
                    wait(dve, s_bc, b * N_MOE + m + 1)
                    if m >= 3:
                        wait(dve, s_dn, b * N_BLK + m)
                    elif not first:
                        wait(dve, s_dn, b * N_BLK)
                    nc.vector.tensor_tensor(hidden[m % 3], act_out[m % 2], banks[:, B + m % 2, :],
                                            ALU.mult).then_inc(s_h, 1)
                    if m == 1 and not first:
                        residual(b - 1)
                    if m == 6:
                        wait(dve, s_pr, b + 1)
                        wait(dve, s_prod, b)
                        nc.vector.tensor_tensor(total, banks[:, G, :], skip_all[:, bass.ds(b * T, T)],
                                                ALU.add).then_inc(s_tot, 1)

            def end(b):
                multiply(b)
                residual(b)

            sequences(dve, body, end)


def kernel(**inputs):
    import numpy as _np
    import concourse.bacc as _bacc
    from concourse import mybir as _mybir
    from concourse.bass_utils import run_bass_kernel_spmd as _run

    a = {k.replace("L0_", ""): _np.asarray(v) for k, v in inputs.items()}
    C = 128
    qkvff = a["attn_w_qkvff"].T
    swap = _np.arange(C) ^ 1
    q, k = qkvff[:, 0:C], qkvff[:, C:2 * C]
    w_up = _np.concatenate([q, q[:, swap], k, k[:, swap], qkvff[:, 2 * C:], a["attn_w_gated"].T, a["ffn_shared_up"],
                            a["ffn_expert_up"].transpose(1, 0, 2).reshape(C, -1)], 1)
    w_down = _np.concatenate([a["ffn_expert_down"].reshape(-1, C), a["ffn_shared_down"], a["attn_w_ff"].T,
                              a["attn_w_proj"].T], 0).reshape(-1, C, C).transpose(1, 0, 2).reshape(C, -1)
    vecs = _np.stack([a["attn_rms_w"], a["attn_gn_w"], a["attn_gn_b"], a["attn_b_gated"], a["attn_b_proj"]], 1)
    x = a["attn_x"]
    arrays = {"x": x.reshape(-1, C), "w_up": w_up, "w_down": w_down, "w_gate": a["ffn_gate_weight"].T, "vecs": vecs}
    arrays.update(shape_tables())
    arrays = {k: _np.ascontiguousarray(v) for k, v in arrays.items()}

    nc = _bacc.Bacc("TRN2", target_bir_lowering=False, num_devices=1)
    args = [nc.dram_tensor(k, v.shape, _mybir.dt.from_np(v.dtype), kind="ExternalInput").ap() for k, v in arrays.items()]
    out = nc.dram_tensor("out", arrays["x"].shape, _mybir.dt.from_np(_np.dtype("float32")), kind="ExternalOutput").ap()
    build(nc, *args, out)
    r = _run(nc, [arrays], core_ids=[0])
    return r.results[0]["out"].reshape(x.shape)
```

```python
from contextlib import ExitStack

import numpy as np

import concourse.bass as bass
from concourse import mybir

P = 128
ALU = mybir.AluOpType
ACT = mybir.ActivationFunctionType
AX = mybir.AxisListType.X
F32 = mybir.dt.float32
F32R = mybir.dt.float32r
F16 = mybir.dt.float16
I32 = mybir.dt.int32

HEADS = 16
HD = 8
GROUPS = 4
CHUNK = 32
T = 512
CHUNKS = T // CHUNK
TILES = T // P
LN_EPS = 1e-5
GN_EPS = 1e-5
EXPERTS = 16
TOP_K = 4
TOPK_GROUP = 2
N_GROUP = 4
ROUTED_SCALING = 2.5

Q, QS, K, KS, V, FF, GATED, SHARED, MOE = 0, 1, 2, 3, 4, 5, 7, 8, 10
N_UP = 18
RMS_BLOCKS = 7
D_MOE, D_SHARED, D_FF, D_PROJ = 0, 8, 10, 12
N_DOWN = 13
N_SPLIT = 10
SCRATCH = 15
XPARTS = 4
PARTS = ((0, 0), (0, 1), (1, 0))
ROUTE_STEPS = 27
FILLER, MARK = -1.0, -3.0


def shape_tables():
    C = P
    t = np.arange(T, dtype=np.float64)
    ch = np.arange(C)
    scale_vec = (np.arange(0, C, 2) + 0.4 * C) / (1.4 * C)
    inv_freq = 1.0 / 10000.0 ** (np.arange(C // 2) / (C // 2))
    angle = t[None, :] * inv_freq[ch // 2][:, None]
    sign = np.where(ch % 2 == 0, -1.0, 1.0)[:, None]
    gamma = 1.0 - 2.0 ** (-5.0 - ch // HD)
    local = np.arange(T) % CHUNK
    base = gamma * scale_vec[ch // 2] ** (1 / 64.0)
    grow = base[:, None] ** (local[None, :] + 1.0)
    cos, sin = np.cos(angle), np.sin(angle) * sign
    rope = np.stack([cos * grow * HD ** -0.5, sin * grow * HD ** -0.5, cos / grow, sin / grow], 1)
    in_group = (ch // HD) % 4
    decay = base ** CHUNK
    col = np.arange(32)
    same_head = in_group[:, None] == (col // HD)[None, :]
    state_mask = same_head * decay[:, None]
    carry = np.repeat(np.repeat(decay[:, None], 32, 1)[:, :, None], CHUNKS, 2)
    carry[:, :, 0] = 0.0
    causal = (ch % CHUNK)[:, None] <= np.arange(CHUNK)[None, :]
    head_of = in_group[:, None] == np.arange(4)[None, :]
    router = np.zeros((P, 8, P))
    for m in range(8):
        for half in range(2):
            for part in range(2):
                router[16 * part + 2 * m + half, m, 64 * half:64 * half + 64] = 1.0
    out = {
        "t_rope": rope.reshape(C, 4 * T), "t_state": state_mask,
        "t_carry": carry.reshape(C, T), "t_causal": causal, "t_head": head_of,
        "t_router": router.reshape(P, 8 * P), "t_ident": np.eye(P),
    }
    return {k: np.ascontiguousarray(v, dtype=np.float32) for k, v in out.items()}


def wait(engine, semaphore, value):
    if not isinstance(value, int) or value > 0:
        engine.wait_ge(semaphore, value)


class Shared:
    pass


def build(nc, x, w_up, w_down, w_gate, vecs, t_rope, t_state, t_carry, t_causal, t_head,
          t_router, t_ident, out):
    rows = x.shape[0]
    NB = rows // T
    NT = rows // P
    g = Shared()
    with ExitStack() as ctx, ExitStack() as early:
        def sb(name, shape, dt=F32):
            return ctx.enter_context(nc.sbuf_tensor(name, shape, dt))

        def sb_early(name, shape, dt=F32):
            return early.enter_context(nc.sbuf_tensor(name, shape, dt))

        def sem(name):
            return ctx.enter_context(nc.semaphore(name))

        g.NB, g.NT = NB, NT
        g.up = up = [sb("up_hi", [P, N_UP * P], F32R), sb("up_lo", [P, N_UP * P], F32R)]
        g.down = down = [sb("down_hi", [P, N_SPLIT * P], F32R), sb("down_lo", [P, N_SPLIT * P], F32R)]
        g.down_whole = sb("down_whole", [P, (N_DOWN - N_SPLIT) * P])
        g.vec = vec = sb("vec", [P, 5])
        g.router = router = sb("router", [P, 8 * P], F32R)
        g.ident = ident = sb("ident", [P, P])
        g.eps = eps = sb("eps", [P, 1])
        g.xn_all = xn_all = sb("xn_all", [P, rows])
        g.y_all = y_all = sb("y_all", [P, rows])
        g.skip_all = skip_all = sb("skip_all", [P, rows])
        g.comb_all = sb("comb_all", [P, NT * EXPERTS])
        g.y_var = sb("y_var", [P, NT * HEADS])
        g.gate_w = sb_early("gate_w", [P, EXPERTS])
        g.rope = rope = sb_early("rope", [P, 4, T])
        g.state_mask = state_mask = sb_early("state_mask", [P, 32])
        g.carry = carry = sb_early("carry", [P, T])
        g.causal = causal = sb_early("causal", [P, CHUNK])
        g.head_of = head_of = sb_early("head_of", [P, 4])
        g.row_mean = row_mean = sb_early("row_mean", [P, NT])
        g.row_rstd = row_rstd = sb_early("row_rstd", [P, NT])
        g.row_rms = row_rms = sb_early("row_rms", [P, NT])
        g.vexp = vexp = sb_early("vexp", [P, CHUNKS * P])
        scratch = sb_early("scratch", [P, SCRATCH * T])

        g.banks = ctx.enter_context(nc.psum_tensor("banks", [P, 8, T], F32))
        g.scratch = scratch
        g.x_rows = x_rows = x.rearrange("(n p) c -> p n c", p=P)
        g.out_rows = out.rearrange("(n p) c -> p n c", p=P)
        seqs = xn_all[:, :].rearrange("p (n c) -> p n c", c=P)

        s_x = [sem(f"x_loaded{i}") for i in range(XPARTS)]
        s_up_raw, s_down_raw = sem("up_loaded"), sem("down_loaded")
        g.s_weights = s_weights = sem("weights_loaded")
        g.s_tables = s_tables = sem("tables_loaded")
        s_rt, s_ctab = sem("router_loaded"), sem("causal_loaded")
        g.s_rope = s_rope = sem("rope_loaded")
        s_eps = sem("eps_set")
        s_bn = sem("bn_done")
        s_step = sem("p_step")
        s_var = sem("variances_ready")
        s_std = sem("deviations_ready")
        s_rms_fold = sem("rms_folded")
        s_amax, s_amax_all = sem("largest_of_partition"), sem("largest_of_all")
        s_fold = sem("weights_folded")
        s_hi = sem("high_parts")
        g.s_split = s_split = sem("weights_split")
        s_tab_scaled = sem("tables_scaled")
        g.s_zero = s_zero = sem("vexp_zeroed")

        up_raw = skip_all[:, 0:N_UP * P]
        router_raw = y_all[:, 0:8 * P]
        down_raw = y_all[:, 8 * P:(8 + N_SPLIT) * P]

        bn = scratch[:, 0:NT * 6]
        small = scratch[:, NT * 6:NT * 6 + 8 * NT]
        two_var = small[:, 0:2 * NT]
        two_std = small[:, 2 * NT:4 * NT]
        mean_sum, mean_gap, nrm = (small[:, i * NT:(i + 1) * NT] for i in (4, 5, 6))
        v_mean = small[:, 7 * NT:7 * NT + HEADS]
        spare = small[:, 7 * NT + HEADS:8 * NT]
        amax, power, inverse, both = spare[:, 0:2], spare[:, 2:4], spare[:, 4:6], spare[:, 6:7]
        amax_all, amin = spare[:, 8:10], spare[:, 10:12]

        with nc.Block() as block:
            @block.sync
            def _(sp):
                n = NT // XPARTS
                for i in range(XPARTS):
                    sp.dma_start(seqs[:, i * n:(i + 1) * n, :], x_rows[:, i * n:(i + 1) * n, :]).then_inc(s_x[i], 16)
                sp.dma_start(down_raw, w_down[:, 0:N_SPLIT * P]).then_inc(s_down_raw, 16)
                sp.dma_start(g.down_whole[:], w_down[:, N_SPLIT * P:]).then_inc(s_weights, 16)
                sp.dma_start(g.gate_w[:], w_gate).then_inc(s_weights, 16)

            @block.scalar
            def _(act):
                act.dma_start(vec[:], vecs).then_inc(s_up_raw, 16)
                act.dma_start(up_raw, w_up).then_inc(s_up_raw, 16)
                act.dma_start(rope[:, :, :], t_rope.rearrange("p (n t) -> p n t", n=4)).then_inc(s_rope, 16)
                act.wait_ge(s_fold, 2)
                nc.scalar.copy(up[0][:, :], up_raw).then_inc(s_hi, 1)
                act.wait_ge(s_down_raw, 16)
                nc.scalar.copy(down[0][:, :], down_raw).then_inc(s_hi, 1)
                act.wait_ge(s_var, 2)
                nc.scalar.activation(two_std, two_var, ACT.Sqrt).then_inc(s_std, 1)

            @block.gpsimd
            def _(pool):
                pool.dma_start(causal[:], t_causal).then_inc(s_ctab, 16)
                pool.dma_start(state_mask[:], t_state).then_inc(s_ctab, 16)
                pool.dma_start(carry[:], t_carry).then_inc(s_tables, 16)
                pool.dma_start(head_of[:], t_head).then_inc(s_tables, 16)
                pool.dma_start(ident[:], t_ident).then_inc(s_tables, 16)
                pool.dma_start(router_raw, t_router).then_inc(s_rt, 16)
                nc.gpsimd.memset(vexp[:, :], 0.0).then_inc(s_zero, 1)
                pool.wait_ge(s_amax, 1)
                nc.gpsimd.partition_all_reduce(amax_all, amax, P, bass.bass_isa.ReduceOp.max).then_inc(s_amax_all, 1)

            @block.vector
            def _(dve):
                steps = [0]

                def step(instruction):
                    instruction.then_inc(s_step, 1)
                    steps[0] += 1
                    dve.wait_ge(s_step, steps[0])

                def statistics(i):
                    dve.wait_ge(s_x[i], 16)
                    per = NT // XPARTS // 8
                    with dve.Fori(i * per, (i + 1) * per) as n:
                        for j in range(8):
                            nc.vector.bn_stats(bn[:, bass.ds(n * 48 + j * 6, 6)],
                                               xn_all[:, bass.ds(n * 8 * P + j * P, P)]).then_inc(s_bn, 1)

                nc.vector.memset(eps[:, :], GN_EPS).then_inc(s_eps, 1)
                statistics(0)
                dve.wait_ge(s_up_raw, 32)
                nc.vector.tensor_scalar(up_raw[:, 0:RMS_BLOCKS * P], up_raw[:, 0:RMS_BLOCKS * P], vec[:, 0:1], None,
                                        ALU.mult).then_inc(s_rms_fold, 1)
                dve.wait_ge(s_rms_fold, 1)
                qk_w = up_raw[:, 0:4 * P].rearrange("p (a b c) -> p a b c", a=2, b=2)[:, :, 0, :]
                nc.vector.tensor_reduce(amax, qk_w, AX, ALU.max).then_inc(s_step, 1)
                steps[0] += 1
                step(nc.vector.tensor_reduce(amin, qk_w, AX, ALU.min))
                nc.vector.scalar_tensor_tensor(amax, amin, -1.0, amax, ALU.mult, ALU.max).then_inc(s_amax, 1)
                v_w = up_raw[:, V * P:(V + 1) * P].rearrange("p (h d) -> p h d", d=HD)
                step(nc.vector.tensor_reduce(v_mean, v_w, AX, ALU.add))
                step(nc.vector.tensor_scalar(v_mean, v_mean, 1.0 / HD, None, ALU.mult))
                nc.vector.tensor_tensor(v_w, v_w, v_mean.unsqueeze(2).broadcast_to([P, HEADS, HD]),
                                        ALU.subtract).then_inc(s_fold, 1)
                statistics(1)
                dve.wait_ge(s_amax_all, 1)
                step(nc.vector.tensor_scalar(power, amax_all, 2.0 ** -60, None, ALU.max))
                step(nc.vector.tensor_scalar(power.bitcast(I32), power.bitcast(I32), 0x7F800000, None, ALU.bitwise_and))
                step(nc.vector.reciprocal(inverse, power))
                nc.vector.tensor_tensor(both, power[:, 0:1], power[:, 1:2], ALU.mult).then_inc(s_step, 1)
                steps[0] += 1
                nc.vector.tensor_scalar(up_raw[:, Q * P:K * P], up_raw[:, Q * P:K * P], inverse[:, 0:1], None, ALU.mult)
                nc.vector.tensor_scalar(up_raw[:, K * P:V * P], up_raw[:, K * P:V * P], inverse[:, 1:2], None,
                                        ALU.mult).then_inc(s_fold, 1)
                dve.wait_ge(s_ctab, 32)
                dve.wait_ge(s_step, steps[0])
                nc.vector.tensor_scalar(causal[:, :], causal[:, :], both, None, ALU.mult).then_inc(s_tab_scaled, 1)
                nc.vector.tensor_scalar(state_mask[:, :], state_mask[:, :], both, None, ALU.mult).then_inc(s_tab_scaled, 1)
                statistics(2)
                dve.wait_ge(s_hi, 1)
                nc.vector.tensor_tensor(up[1][:, :], up_raw, up[0][:, :].bitcast(F32), ALU.subtract).then_inc(s_split, 1)
                statistics(3)
                dve.wait_ge(s_bn, NT)
                b = bn.rearrange("p (n s) -> p n s", s=6)
                var, var_eps = two_var[:, NT:2 * NT], two_var[:, 0:NT]
                nc.vector.tensor_tensor(mean_sum, b[:, :, 1], b[:, :, 4], ALU.add).then_inc(s_step, 1)
                nc.vector.tensor_tensor(mean_gap, b[:, :, 1], b[:, :, 4], ALU.subtract).then_inc(s_step, 1)
                steps[0] += 2
                step(nc.vector.tensor_tensor(var_eps, b[:, :, 2], b[:, :, 5], ALU.add))
                nc.vector.tensor_scalar(row_mean[:, :], mean_sum, 0.5, None, ALU.mult).then_inc(s_step, 1)
                steps[0] += 1
                step(nc.vector.scalar_tensor_tensor(mean_gap, mean_gap, 0.25, mean_gap, ALU.mult, ALU.mult))
                nc.vector.scalar_tensor_tensor(var, var_eps, 1.0 / P, mean_gap, ALU.mult, ALU.add).then_inc(s_var, 1)
                dve.wait_ge(s_var, 1)
                nc.vector.tensor_scalar(var_eps, var, LN_EPS, None, ALU.add).then_inc(s_var, 1)
                dve.wait_ge(s_hi, 2)
                nc.vector.tensor_tensor(down[1][:, :], down_raw, down[0][:, :].bitcast(F32), ALU.subtract).then_inc(s_split, 1)
                dve.wait_ge(s_rt, 16)
                nc.vector.tensor_copy(router[:, :], router_raw).then_inc(s_split, 1)
                dve.wait_ge(s_std, 1)
                step(nc.vector.reciprocal(row_rstd[:, :], two_std[:, 0:NT]))
                step(nc.vector.tensor_tensor(nrm, two_std[:, NT:2 * NT], row_rstd[:, :], ALU.mult))
                step(nc.vector.tensor_scalar(nrm, nrm, 1e-8, None, ALU.max))
                step(nc.vector.reciprocal(mean_sum, nrm))
                step(nc.vector.tensor_tensor(row_rms[:, :], mean_sum, row_rstd[:, :], ALU.mult))
                dve.wait_ge(s_tab_scaled, 2)

        attend(nc, sem, g)
        early.close()
        combine(nc, sem, g)


def attend(nc, sem, g):
    with ExitStack() as ctx:
        attend_in(nc, sem, g, lambda name, shape, dt=F32: ctx.enter_context(nc.sbuf_tensor(name, shape, dt)))


def attend_in(nc, sem, g, sb):
    NB, banks, up, down = g.NB, g.banks, g.up, g.down_whole
    xn_all, y_all, skip_all, comb_all, y_var = g.xn_all, g.y_all, g.skip_all, g.comb_all, g.y_var
    ident, rope, vec, vexp = g.ident, g.rope, g.vec, g.vexp

    def part(at, count=1):
        return g.scratch[:, at * T:(at + count) * T]

    xn, xn_t = part(0), part(1)
    ff = part(2, 2)
    xs = part(3)
    cosine, sine = part(4), part(5)
    q_t, k_t = part(6), part(7)
    k_rows, v_rows = part(8), part(9)
    probs = part(10, 4)
    u_in = y_sq = part(14)
    states = sb("states", [P, T])[:, :]
    xs_t = [sb("xs_t_hi", [P, T], F32R)[:, :], sb("xs_t_lo", [P, T], F32R)[:, :]]
    q_16 = sb("q_16", [P, 2, T], F16)
    k_16 = sb("k_16", [P, 2, T], F16)
    k_heads = sb("k_heads", [P, 2, 4 * T], F16)
    SLOTS = EXPERTS + 4
    score = sb("score", [P, TILES * EXPERTS])[:, :]
    pairs = sb("pairs", [P, 4, TILES * N_GROUP])
    kept = sb("kept", [P, TILES, SLOTS])
    marked = sb("marked", [P, TILES, SLOTS])
    largest = sb("largest", [P, TILES, 8])

    s_norm = sem("a_rows_normed")
    s_tr = sem("a_transposed")
    s_xnt = sem("a_xn_t_ready")
    s_xst = sem("a_xs_t_ready")
    s_keep = sem("a_xn_t_kept")
    s_gate = sem("a_logits_ready")
    s_score = sem("a_gate_scores_ready")
    s_route = sem("a_route_step")
    s_filled = sem("a_fillers_set")
    s_ffup = sem("a_ff_up_done")
    s_gelu = sem("a_gelu_ready")
    s_ffdn = sem("a_ff_down_done")
    s_skip = sem("a_skip_kept")
    s_kp = sem("a_k_projected")
    s_kr = sem("a_k_rotated")
    s_kt = sem("a_k_t_ready")
    s_kp16 = sem("a_k_parts")
    s_kl16 = sem("a_k_low_part")
    s_kh = sem("a_k_heads_ready")
    s_qp = sem("a_q_projected")
    s_qr = sem("a_q_rotated")
    s_qt = sem("a_q_t_ready")
    s_qp16 = sem("a_q_high_part")
    s_ql16 = sem("a_q_low_part")
    s_vp = sem("a_v_projected")
    s_vr = sem("a_v_rows_ready")
    s_vx = sem("a_v_expanded")
    s_ktr = sem("a_k_transposed")
    s_krow = sem("a_k_rows_ready")
    s_u = sem("a_updates_done")
    s_um = sem("a_updates_masked")
    s_st = sem("a_states_ready")
    s_sc = sem("a_scores_done")
    s_p = sem("a_probs_ready")
    s_y = sem("a_y_done")
    s_yk = sem("a_y_kept")
    s_yv = sem("a_y_variances")
    s_split, s_weights, s_tables, s_zero = g.s_split, g.s_weights, g.s_tables, g.s_zero

    def split_matmul(out, block, rhs, start=True):
        for i, (a, c) in enumerate(PARTS):
            last = nc.tensor.matmul(out, up[a][:, block * P:(block + 1) * P], rhs[c],
                                    start=start and i == 0, stop=i == 2)
        return last

    with nc.Block() as block:
        @block.sync
        def _(sp):
            with sp.Fori(0, NB) as b:
                wait(sp, s_xnt, b + 1)
                wait(sp, s_norm, b + 1)
                sp.dma_start(xn_all[:, bass.ds(b * T, T)], xn_t).then_inc(s_keep, 16)
            sp.wait_ge(s_keep, 16 * NB)

        @block.tensor
        def _(pe):
            pe.wait_ge(s_split, 3)
            pe.wait_ge(s_weights, 32)
            pe.wait_ge(s_tables, 48)

            def transposes(b):
                wait(pe, s_norm, b + 1)
                wait(pe, s_vr, b)
                wait(pe, s_krow, b)
                for j in range(TILES):
                    nc.tensor.transpose(banks[:, 4, j * P:(j + 1) * P], xn[:, j * P:(j + 1) * P], ident[:, :])
                for j in range(TILES):
                    last = nc.tensor.transpose(banks[:, 5, j * P:(j + 1) * P], xs[:, j * P:(j + 1) * P], ident[:, :])
                last.then_inc(s_tr, 1)

            def feed_forward_up(b):
                wait(pe, s_xst, 2 * b + 2)
                wait(pe, s_skip, b)
                wait(pe, s_score, b)
                for k in range(2):
                    split_matmul(banks[:, 6 + k, :], FF + k, xs_t).then_inc(s_ffup, 1)

            def project_k(b):
                wait(pe, s_xnt, b + 1)
                split_matmul(banks[:, 4, :], K, xs_t)
                split_matmul(banks[:, 5, :], KS, xs_t).then_inc(s_kp, 1)

            def feed_forward_down(b):
                for k in range(2):
                    last = nc.tensor.matmul(banks[:, 6, :], down[:, k * P:(k + 1) * P],
                                            ff[:, k * T:(k + 1) * T], start=k == 0, stop=k == 1)
                last.then_inc(s_ffdn, 1)

            def gate(b):
                wait(pe, s_gelu, 2 * b + 2)
                for j in range(TILES):
                    last = nc.tensor.matmul(banks[:, 7, j * EXPERTS:(j + 1) * EXPERTS], xn_t[:, j * P:(j + 1) * P],
                                            g.gate_w[:, :], start=True, stop=True)
                last.then_inc(s_gate, 1)

            def project_q(b):
                wait(pe, s_kr, 2 * b + 2)
                split_matmul(banks[:, 4, :], Q, xs_t)
                split_matmul(banks[:, 5, :], QS, xs_t).then_inc(s_qp, 1)

            def project_v(b):
                wait(pe, s_qr, 2 * b + 2)
                for j in range(TILES):
                    for i, (a, c) in enumerate(PARTS):
                        last = nc.tensor.matmul(banks[:, 4, j * P:(j + 1) * P], xs_t[a][:, j * P:(j + 1) * P],
                                                up[c][:, V * P:(V + 1) * P], start=i == 0, stop=i == 2)
                last.then_inc(s_vp, 1)

            def k_by_rows(b):
                wait(pe, s_kt, b + 1)
                for j in range(TILES):
                    last = nc.tensor.transpose(banks[:, 5, j * P:(j + 1) * P], k_t[:, j * P:(j + 1) * P], ident[:, :])
                last.then_inc(s_ktr, 1)

            def wait_for_state_updates(b):
                wait(pe, s_krow, b + 1)
                wait(pe, s_vr, b + 1)
                wait(pe, s_yk, 2 * b)

            def state_updates(b):
                for j in range(TILES):
                    for c in range(4):
                        for h in range(GROUPS):
                            rows = slice(32 * c, 32 * c + 32)
                            cols = slice(j * P + 32 * h, j * P + 32 * h + 32)
                            last = nc.tensor.matmul(banks[32 * h:32 * h + 32, c, 32 * j:32 * j + 32],
                                                    k_rows[rows, cols], v_rows[rows, cols], start=True, stop=True)
                last.then_inc(s_u, 1)

            def scores(b):
                wait(pe, s_kh, b + 1)
                wait(pe, s_qp16, b + 1)
                wait(pe, s_ql16, b + 1)
                wait(pe, s_um, b + 1)
                for n in range(CHUNKS):
                    for h in range(GROUPS):
                        rows, cols = slice(32 * h, 32 * h + 32), slice(CHUNK * n, CHUNK * n + CHUNK)
                        for i, (a, c) in enumerate(PARTS):
                            last = nc.tensor.matmul(banks[:, h, cols], k_heads[rows, a, n * P:(n + 1) * P],
                                                    q_16[rows, c, cols], start=i == 0, stop=i == 2)
                last.then_inc(s_sc, 1)

            def outputs(b):
                wait(pe, s_st, b + 1)
                wait(pe, s_vx, b + 1)
                wait(pe, s_p, 4 * b + 4)
                pr = probs.rearrange("p (h t) -> p h t", h=GROUPS)
                for n in range(CHUNKS):
                    j, c = n // 4, n % 4
                    for h in range(GROUPS):
                        nc.tensor.matmul(banks[32 * c:32 * c + 32, h, 32 * j:32 * j + 32],
                                         pr[:, h, CHUNK * n:CHUNK * n + CHUNK],
                                         vexp[:, n * P + 32 * h:n * P + 32 * h + 32],
                                         start=j == 0, stop=n == 0, skip_group_check=True)
                st = states.rearrange("p (e n) -> p e n", n=CHUNKS)
                for n in range(1, CHUNKS):
                    j, c = n // 4, n % 4
                    for h in range(GROUPS):
                        rows = slice(32 * h, 32 * h + 32)
                        last = nc.tensor.matmul(banks[32 * c:32 * c + 32, h, 32 * j:32 * j + 32],
                                                q_t[rows, CHUNK * n:CHUNK * n + CHUNK], st[rows, :, n - 1],
                                                start=False, stop=True, skip_group_check=True)
                last.then_inc(s_y, 1)

            def front_before_outputs(b):
                feed_forward_up(b)
                project_k(b)
                gate(b)
                feed_forward_down(b)

            def front_after_outputs(b):
                project_q(b)
                project_v(b)
                k_by_rows(b)

            transposes(0)
            front_before_outputs(0)
            front_after_outputs(0)

            def body(b):
                wait_for_state_updates(b)
                transposes(b + 1)
                state_updates(b)
                scores(b)
                front_before_outputs(b + 1)
                outputs(b)
                front_after_outputs(b + 1)

            body(0)
            with pe.Fori(1, NB - 1) as b:
                body(b)
            wait_for_state_updates(NB - 1)
            pe.wait_ge(s_skip, NB)
            nc.tensor.transpose(banks[:, 6, 0:P], xn[:, 0:P], ident[:, :])
            state_updates(NB - 1)
            scores(NB - 1)
            outputs(NB - 1)

        @block.scalar
        def _(act):
            vx = vexp[:, :].rearrange("p (j c g h e) -> p j c g h e", j=TILES, c=4, g=GROUPS, h=4)
            vr = v_rows.rearrange("p (j g h e) -> p j g h e", j=TILES, g=GROUPS, h=4)

            def x_by_channels(b):
                wait(act, s_tr, b + 1)
                wait(act, s_keep, b * 16)
                wait(act, s_gate, b)
                wait(act, s_skip, b)
                wait(act, s_vp, b)
                nc.scalar.copy(xs_t[0], banks[:, 5, :]).then_inc(s_xst, 1)
                nc.scalar.copy(xn_t, banks[:, 4, :]).then_inc(s_xnt, 1)

            def gelu(b):
                wait(act, s_ffdn, b)
                for k in range(2):
                    wait(act, s_ffup, 2 * b + k + 1)
                    nc.scalar.activation(ff[:, k * T:(k + 1) * T], banks[:, 6 + k, :], ACT.Gelu).then_inc(s_gelu, 1)

            def gate_scores(b):
                wait(act, s_gate, b + 1)
                wait(act, s_route, b * ROUTE_STEPS)
                nc.scalar.activation(score, banks[:, 7, 0:TILES * EXPERTS], ACT.Sigmoid).then_inc(s_score, 1)

            def high_part_k(b):
                wait(act, s_kt, b + 1)
                wait(act, s_kh, b)
                nc.scalar.copy(k_16[:, 0, :], k_t).then_inc(s_kp16, 1)

            def high_part_q(b):
                wait(act, s_qt, b + 1)
                wait(act, s_sc, b)
                nc.scalar.copy(q_16[:, 0, :], q_t).then_inc(s_qp16, 1)

            def rows_of_v_and_k(b):
                wait(act, s_vp, b + 1)
                wait(act, s_u, b)
                nc.scalar.copy(v_rows, banks[:, 4, :]).then_inc(s_vr, 1)
                wait(act, s_ktr, b + 1)
                nc.scalar.copy(k_rows, banks[:, 5, :]).then_inc(s_krow, 1)

            def expand_v(b):
                wait(act, s_vr, b + 1)
                wait(act, s_y, b)
                for h in range(4):
                    for c in range(4):
                        last = nc.scalar.copy(vx[32 * h:32 * h + 32, :, c, :, h, :], vr[32 * c:32 * c + 32, :, :, h, :])
                last.then_inc(s_vx, 1)

            def keep_y(b):
                wait(act, s_y, b + 1)
                y_b = banks[:, 0:4, 0:P].rearrange("p g (j e) -> p j g e", j=TILES)
                nc.scalar.copy(y_all[:, bass.ds(b * T, T)].rearrange("p (j g e) -> p j g e", j=TILES, g=GROUPS),
                               y_b).then_inc(s_yk, 1)
                wait(act, s_st, b + 1)
                nc.scalar.activation(y_sq.rearrange("p (j g e) -> p j g e", j=TILES, g=GROUPS),
                                     y_b, ACT.Square).then_inc(s_yk, 1)

            act.wait_ge(s_zero, 1)
            x_by_channels(0)
            gelu(0)
            gate_scores(0)
            high_part_k(0)
            high_part_q(0)
            rows_of_v_and_k(0)

            def body(b):
                x_by_channels(b + 1)
                expand_v(b)
                gelu(b + 1)
                gate_scores(b + 1)
                high_part_k(b + 1)
                keep_y(b)
                high_part_q(b + 1)
                rows_of_v_and_k(b + 1)

            body(0)
            with act.Fori(1, NB - 1) as b:
                body(b)
            expand_v(NB - 1)
            keep_y(NB - 1)

        @block.vector
        def _(dve):
            row_mean, row_rstd, row_rms = g.row_mean, g.row_rstd, g.row_rms

            def norm_rows(b):
                wait(dve, s_tr, b)
                wait(dve, s_ffdn, b)
                for j in range(TILES):
                    tile = xn_all[:, bass.ds(b * T + j * P, P)]
                    mean = row_mean[:, bass.ds(b * TILES + j, 1)]
                    nc.vector.tensor_scalar(xn[:, j * P:(j + 1) * P], tile, mean,
                                            row_rstd[:, bass.ds(b * TILES + j, 1)], ALU.subtract, ALU.mult)
                    last = nc.vector.tensor_scalar(xs[:, j * P:(j + 1) * P], tile, mean,
                                                   row_rms[:, bass.ds(b * TILES + j, 1)], ALU.subtract, ALU.mult)
                last.then_inc(s_norm, 1)

            def split_x(b):
                wait(dve, s_xst, 2 * b + 1)
                nc.vector.tensor_tensor(xs_t[1], banks[:, 5, :], xs_t[0].bitcast(F32), ALU.subtract).then_inc(s_xst, 1)

            def rotate(b, s_projected, s_rotated, at):
                wait(dve, s_projected, b + 1)
                if at == 0:
                    wait(dve, s_kt, b + 1)
                else:
                    wait(dve, s_qt, b)
                nc.vector.tensor_tensor(cosine, banks[:, 4, :], rope[:, at, :], ALU.mult).then_inc(s_rotated, 1)
                nc.vector.tensor_tensor(sine, banks[:, 5, :], rope[:, at + 1, :], ALU.mult).then_inc(s_rotated, 1)

            def expand_k(b):
                wait(dve, s_kp16, b + 1)
                wait(dve, s_kl16, b + 1)
                wait(dve, s_sc, b)
                heads = k_heads[:, :, :].rearrange("p w (n h s) -> p (w n) h s", h=4, s=CHUNK)
                k_chunks = k_16[:, :, :].rearrange("p w (n s) -> p (w n) s", s=CHUNK)
                for h in range(4):
                    last = nc.vector.tensor_scalar(heads[:, :, h, :], k_chunks, g.head_of[:, h:h + 1], None, ALU.mult)
                last.then_inc(s_kh, 1)

            def keep_skip(b):
                wait(dve, s_ffdn, b + 1)
                wait(dve, s_xnt, b + 1)
                nc.vector.scalar_tensor_tensor(skip_all[:, bass.ds(b * T, T)], banks[:, 6, :], vec[:, 4:5], xn_t,
                                               ALU.add, ALU.add).then_inc(s_skip, 1)

            def carry_states(b):
                wait(dve, s_u, b + 1)
                wait(dve, s_st, b)
                wait(dve, s_yv, b)
                nc.vector.tensor_tensor(u_in.rearrange("p (e j c) -> p j c e", e=32, j=TILES),
                                        banks[:, 0:4, 0:P].rearrange("p c (j e) -> p j c e", j=TILES),
                                        g.state_mask[:, :].unsqueeze(1).unsqueeze(1).broadcast_to([P, TILES, 4, 32]),
                                        ALU.mult).then_inc(s_um, 1)
                wait(dve, s_um, b + 1)
                wait(dve, s_y, b)
                nc.vector.tensor_tensor_scan(states, g.carry[:, :], u_in, 0.0, ALU.mult, ALU.add).then_inc(s_st, 1)

            def mask_scores(b):
                wait(dve, s_sc, b + 1)
                wait(dve, s_y, b)
                for h in range(GROUPS):
                    nc.vector.tensor_tensor(probs[:, h * T:(h + 1) * T].rearrange("p (n t) -> p n t", t=CHUNK),
                                            banks[:, h, :].rearrange("p (n t) -> p n t", t=CHUNK),
                                            g.causal[:, :].unsqueeze(1).broadcast_to([P, CHUNKS, CHUNK]),
                                            ALU.mult).then_inc(s_p, 1)

            def variances(b):
                wait(dve, s_yk, 2 * b + 2)
                nc.vector.tensor_reduce(y_var[:, bass.ds(b * (TILES * HEADS), TILES * HEADS)],
                                        y_sq.rearrange("p (h e) -> p h e", e=HD), AX, ALU.add).then_inc(s_yv, 1)

            def choose_groups(b):
                steps = [b * ROUTE_STEPS, 0]

                def step(instruction):
                    instruction.then_inc(s_route, 1)
                    steps[1] += 1
                    dve.wait_ge(s_route, steps[0] + steps[1])

                wait(dve, s_score, b + 1)
                s4 = score.rearrange("p (g e) -> p g e", e=4)
                f = [pairs[:, i, :] for i in range(4)]
                nc.vector.tensor_tensor(f[0], s4[:, :, 0], s4[:, :, 1], ALU.max)
                nc.vector.tensor_tensor(f[1], s4[:, :, 0], s4[:, :, 1], ALU.min)
                nc.vector.tensor_tensor(f[2], s4[:, :, 2], s4[:, :, 3], ALU.max)
                step(nc.vector.tensor_tensor(f[3], s4[:, :, 2], s4[:, :, 3], ALU.min))
                step(nc.vector.tensor_tensor(f[1], f[1], f[3], ALU.max))
                step(nc.vector.tensor_tensor(f[3], f[0], f[2], ALU.min))
                step(nc.vector.tensor_tensor(f[1], f[1], f[3], ALU.max))
                step(nc.vector.tensor_tensor(f[0], f[0], f[2], ALU.max))
                step(nc.vector.tensor_tensor(f[0], f[0], f[1], ALU.add))
                sums, rank, wins = (f[i].rearrange("p (t g) -> p t g", g=N_GROUP) for i in range(3))
                step(nc.vector.memset(rank, 0.0))
                for off in range(1, N_GROUP):
                    lo, hi = slice(0, N_GROUP - off), slice(off, N_GROUP)
                    step(nc.vector.tensor_tensor(wins[:, :, lo], sums[:, :, lo], sums[:, :, hi], ALU.is_ge))
                    step(nc.vector.tensor_tensor(rank[:, :, hi], rank[:, :, hi], wins[:, :, lo], ALU.add))
                    step(nc.vector.scalar_tensor_tensor(rank[:, :, lo], rank[:, :, lo], 1.0, wins[:, :, lo],
                                                        ALU.add, ALU.subtract))
                step(nc.vector.tensor_scalar(f[3], f[1], float(TOPK_GROUP) - 0.5, None, ALU.is_lt))
                part_of = f[3].rearrange("p (t g) -> p t g", g=N_GROUP).unsqueeze(3).broadcast_to([P, TILES, N_GROUP, 4])
                step(nc.vector.tensor_tensor(kept[:, :, 0:EXPERTS].rearrange("p t (g e) -> p t g e", e=4),
                                             score.rearrange("p (t g e) -> p t g e", g=N_GROUP, e=4), part_of, ALU.mult))
                return steps[1]

            def choose_experts(b, done):
                steps = [b * ROUTE_STEPS, done]

                def step(instruction):
                    instruction.then_inc(s_route, 1)
                    steps[1] += 1
                    dve.wait_ge(s_route, steps[0] + steps[1])

                total, inverse, tiny = (pairs[:, i, 0:TILES] for i in range(3))
                for j in range(TILES):
                    last = nc.vector.max(largest[:, j, :], kept[:, j, 0:EXPERTS])
                step(last)
                step(nc.vector.memset(largest[:, :, TOP_K:8], FILLER))
                nc.vector.memset(tiny, 1e-20)
                for j in range(TILES):
                    last = nc.vector.match_replace(marked[:, j, :], largest[:, j, :], kept[:, j, :], MARK)
                step(last)
                chosen = kept[:, :, 0:EXPERTS]
                step(nc.vector.scalar_tensor_tensor(chosen, marked[:, :, 0:EXPERTS], MARK / 2 + FILLER / 2,
                                                    score.rearrange("p (t e) -> p t e", e=EXPERTS), ALU.is_lt, ALU.mult))
                step(nc.vector.tensor_reduce(total, chosen, AX, ALU.add))
                step(nc.vector.tensor_tensor(total, total, tiny, ALU.add))
                step(nc.vector.reciprocal(inverse, total))
                step(nc.vector.tensor_scalar(inverse, inverse, ROUTED_SCALING, None, ALU.mult))
                step(nc.vector.tensor_tensor(comb_all[:, bass.ds(b * (TILES * EXPERTS), TILES * EXPERTS)].rearrange(
                    "p (t e) -> p t e", e=EXPERTS), chosen, inverse.unsqueeze(2).broadcast_to([P, TILES, EXPERTS]), ALU.mult))
                assert steps[1] == ROUTE_STEPS, steps[1]

            nc.vector.memset(kept[:, :, EXPERTS:SLOTS], FILLER).then_inc(s_filled, 1)
            norm_rows(0)
            split_x(0)
            dve.wait_ge(s_tables, 48)
            dve.wait_ge(g.s_rope, 16)
            dve.wait_ge(s_filled, 1)
            rotate(0, s_kp, s_kr, 2)
            keep_skip(0)
            rotate(0, s_qp, s_qr, 0)
            expand_k(0)
            choose_experts(0, choose_groups(0))
            norm_rows(1)

            def body(b):
                carry_states(b)
                split_x(b + 1)
                mask_scores(b)
                rotate(b + 1, s_kp, s_kr, 2)
                done = choose_groups(b + 1)
                keep_skip(b + 1)
                expand_k(b + 1)
                choose_experts(b + 1, done)
                rotate(b + 1, s_qp, s_qr, 0)
                variances(b)

            body(0)
            norm_rows(2)
            with dve.Fori(1, NB - 2) as b:
                body(b)
                norm_rows(b + 2)
            body(NB - 2)
            carry_states(NB - 1)
            mask_scores(NB - 1)
            variances(NB - 1)

        @block.gpsimd
        def _(pool):
            def sum_k(b):
                wait(pool, s_kr, 2 * b + 2)
                wait(pool, s_ktr, b)
                wait(pool, s_kl16, b)
                nc.gpsimd.tensor_tensor(k_t, cosine, sine, ALU.add).then_inc(s_kt, 1)
                wait(pool, s_kp16, b + 1)
                wait(pool, s_kh, b)
                nc.gpsimd.tensor_tensor(k_16[:, 1, :], k_t, k_16[:, 0, :], ALU.subtract).then_inc(s_kl16, 1)

            def sum_q(b):
                wait(pool, s_qr, 2 * b + 2)
                wait(pool, s_y, b)
                nc.gpsimd.tensor_tensor(q_t, cosine, sine, ALU.add).then_inc(s_qt, 1)
                wait(pool, s_qp16, b + 1)
                wait(pool, s_sc, b)
                nc.gpsimd.tensor_tensor(q_16[:, 1, :], q_t, q_16[:, 0, :], ALU.subtract).then_inc(s_ql16, 1)

            pool.wait_ge(s_tables, 48)
            sum_k(0)
            sum_q(0)
            with pool.Fori(1, NB) as b:
                sum_k(b)
                sum_q(b)


def combine(nc, sem, g):
    with ExitStack() as ctx:
        combine_in(nc, sem, g, lambda name, shape, dt=F32: ctx.enter_context(nc.sbuf_tensor(name, shape, dt)))


def combine_in(nc, sem, g, sb):
    NB, banks, up, down, router = g.NB, g.banks, g.up, g.down, g.router
    xn_all, y_all, skip_all = g.xn_all, g.y_all, g.skip_all
    comb_all, y_std, vec, ident = g.comb_all, g.y_var, g.vec, g.ident
    x_rows, out_rows = g.x_rows, g.out_rows

    def buffers(name, count, dt=F32):
        return [sb(f"{name}{i}", [P, T], dt)[:, :] for i in range(count)]

    x_t = buffers("x_t", 2, F32R)
    comb_t = sb("comb_t", [P, T], F32R)[:, :]
    yn, y_t, gated, y_gated, total, silu_ffn, product, x_in, result = buffers("c_rows", 9)
    act_out = buffers("act_out", 2)
    hidden = buffers("hidden", 2)
    hidden_hi = buffers("hidden_hi", 5, F32R)
    hidden_lo = buffers("hidden_lo", 5, F32R)
    comb_parts = sb("comb_parts", [P, TILES * 2 * EXPERTS])[:, :]
    y_rstd = sb("y_rstd", [P, TILES * HEADS])[:, :]
    N_MOE, N_SH = 8, 2
    N_BLK = N_MOE + N_SH
    U, B, O, G, YT, CT = 0, 2, 4, 5, 6, 7

    s_zero = sem("c_comb_t_zeroed")
    s_std = sem("c_y_deviations")
    s_xhi, s_xlo = sem("c_x_hi"), sem("c_x_lo")
    s_cp = sem("c_comb_parts")
    s_ct = sem("c_comb_transposed")
    s_ctr = sem("c_comb_t_ready")
    s_rstd = sem("c_y_rstd")
    s_yn = sem("c_y_normed")
    s_ytr = sem("c_y_transposed")
    s_yt = sem("c_y_t_ready")
    s_gp = sem("c_gate_projected")
    s_gs = sem("c_gate_ready")
    s_yg = sem("c_y_gated")
    s_pr = sem("c_y_projected")
    s_tot = sem("c_branch_ready")
    s_up = sem("c_up_done")
    s_silu = sem("c_silu_ready")
    s_bc = sem("c_weights_spread")
    s_h = sem("c_hidden_weighted")
    s_hi = sem("c_hidden_high_part")
    s_lo = sem("c_hidden_low_part")
    s_dn = sem("c_down_done")
    s_g = sem("c_ffn_silu_ready")
    s_prod = sem("c_product_ready")
    s_bt = sem("c_product_by_rows")
    s_res = sem("c_result_ready")
    s_xin = sem("c_x_loaded")
    s_out = sem("c_out_stored")

    def sequences(engine, body, end=None):
        body(0, True)
        body(1, False)
        with engine.Fori(2, NB) as b:
            body(b, False)
        if end is not None:
            end(NB - 1)

    with nc.Block() as block:
        @block.sync
        def _(sp):
            def body(b, first):
                if not first:
                    wait(sp, s_res, b)
                sp.dma_start(x_in.rearrange("p (j c) -> p j c", c=P), x_rows[:, bass.ds(b * TILES, TILES), :]
                             ).then_inc(s_xin, 16)
            sequences(sp, body)

        @block.gpsimd
        def _(pool):
            def store(b):
                wait(pool, s_res, b + 1)
                pool.dma_start(out_rows[:, bass.ds(b * TILES, TILES), :], result.rearrange("p (j c) -> p j c", c=P)
                               ).then_inc(s_out, 16)

            def low_part(b, k):
                wait(pool, s_hi, b * N_BLK + k + 1)
                wait(pool, s_dn, b * N_BLK + k - 4)
                nc.gpsimd.tensor_tensor(hidden_lo[k % 5], hidden[k % 2], hidden_hi[k % 5].bitcast(F32),
                                        ALU.subtract).then_inc(s_lo, 1)

            def body(b, first):
                low_part(b, 0)
                low_part(b, 1)
                wait(pool, s_gs, b + 1)
                wait(pool, s_yt, b + 1)
                if not first:
                    wait(pool, s_pr, b)
                nc.gpsimd.tensor_tensor(y_gated, gated, y_t, ALU.mult).then_inc(s_yg, 1)
                for k in range(2, N_BLK):
                    low_part(b, k)
                    if k == 5 and not first:
                        store(b - 1)
            sequences(pool, body, store)
            pool.wait_ge(s_out, 16 * NB)

        @block.tensor
        def _(pe):
            pe.wait_ge(s_zero, 1)

            def by_rows(b):
                wait(pe, s_prod, b + 1)
                for j in range(TILES):
                    last = nc.tensor.transpose(banks[:, CT, j * P:(j + 1) * P], product[:, j * P:(j + 1) * P], ident[:, :])
                last.then_inc(s_bt, 1)

            def split_matmul(out, block, rhs):
                for i, (a, c) in enumerate(PARTS):
                    last = nc.tensor.matmul(out, up[a][:, block * P:(block + 1) * P], rhs[c], start=i == 0, stop=i == 2)
                return last

            def block_up(b, k):
                wait(pe, s_silu, b * N_BLK + k - 1)
                split_matmul(banks[:, U + k % 2, :], SHARED + k, x_t).then_inc(s_up, 1)

            def spread(b, first, m):
                if not (first and m < 2):
                    wait(pe, s_h, b * N_MOE + m - 1)
                nc.tensor.matmul(banks[:, B + m % 2, :], router[:, m * P:(m + 1) * P], comb_t,
                                 start=True, stop=True).then_inc(s_bc, 1)

            def block_down(b, k):
                wait(pe, s_lo, b * N_BLK + k + 1)
                at = D_SHARED + k if k < N_SH else D_MOE + k - N_SH
                rhs = (hidden_hi[k % 5], hidden_lo[k % 5])
                for i, (a, c) in enumerate(PARTS):
                    last = nc.tensor.matmul(banks[:, O, :], down[a][:, at * P:(at + 1) * P], rhs[c],
                                            start=k == 0 and i == 0, stop=k == N_BLK - 1 and i == 2)
                last.then_inc(s_dn, 1)

            def last_blocks(b):
                block_down(b, N_BLK - 1)

            def body(b, first):
                wait(pe, s_xhi, b + 1)
                wait(pe, s_xlo, b + 1)
                block_up(b, 0)
                if not first:
                    block_down(b - 1, N_BLK - 2)
                block_up(b, 1)
                wait(pe, s_cp, 2 * b + 2)
                if not first:
                    wait(pe, s_res, b - 1)
                for j in range(TILES):
                    last = nc.tensor.transpose(banks[0:2 * EXPERTS, CT, j * P:(j + 1) * P],
                                               comb_parts[:, j * 2 * EXPERTS:(j + 1) * 2 * EXPERTS], ident[:, :])
                last.then_inc(s_ct, 1)
                if not first:
                    last_blocks(b - 1)
                    wait(pe, s_tot, b)
                split_matmul(banks[:, G, :], GATED, x_t).then_inc(s_gp, 1)
                block_up(b, 2)
                wait(pe, s_ctr, b + 1)
                spread(b, first, 0)
                wait(pe, s_yn, b + 1)
                if not first:
                    wait(pe, s_yt, b)
                for j in range(TILES):
                    last = nc.tensor.transpose(banks[:, YT, j * P:(j + 1) * P], yn[:, j * P:(j + 1) * P], ident[:, :])
                last.then_inc(s_ytr, 1)
                block_up(b, 3)
                spread(b, first, 1)
                if not first:
                    wait(pe, s_g, b)
                block_down(b, 0)
                if not first:
                    by_rows(b - 1)
                for k in range(4, N_BLK):
                    block_up(b, k)
                    block_down(b, k - 3)
                    spread(b, first, k - 2)
                    if k == 7:
                        wait(pe, s_yg, b + 1)
                        nc.tensor.matmul(banks[:, G, :], g.down_whole[:, 2 * P:3 * P], y_gated,
                                         start=True, stop=True).then_inc(s_pr, 1)
                block_down(b, N_BLK - 3)

            def end(b):
                block_down(b, N_BLK - 2)
                block_down(b, N_BLK - 1)
                by_rows(b)

            sequences(pe, body, end)

        @block.scalar
        def _(act):
            nc.scalar.activation(y_std[:, :], y_std[:, :], ACT.Sqrt, bias=g.eps[:, 0:1], scale=1.0 / HD).then_inc(s_std, 1)

            def block_silu(b, first, k):
                wait(act, s_up, b * N_BLK + k + 1)
                if k < N_SH:
                    wait(act, s_lo, b * N_BLK + k - 1)
                    nc.scalar.activation(hidden[k % 2], banks[:, U + k % 2, :], ACT.Silu).then_inc(s_silu, 1)
                else:
                    m = k - N_SH
                    if not (first and m < 2):
                        wait(act, s_h, b * N_MOE + m - 1)
                    nc.scalar.activation(act_out[m % 2], banks[:, U + k % 2, :], ACT.Silu).then_inc(s_silu, 1)

            def high_part(b, k):
                if k < N_SH:
                    wait(act, s_silu, b * N_BLK + k + 1)
                else:
                    wait(act, s_h, b * N_MOE + k - N_SH + 1)
                wait(act, s_dn, b * N_BLK + k - 4)
                nc.scalar.copy(hidden_hi[k % 5], hidden[k % 2]).then_inc(s_hi, 1)

            def silu_of_sum(b):
                wait(act, s_dn, b * N_BLK + N_BLK)
                wait(act, s_prod, b)
                nc.scalar.activation(silu_ffn, banks[:, O, :], ACT.Silu).then_inc(s_g, 1)

            def body(b, first):
                wait(act, s_up, b * N_BLK)
                wait(act, s_gp, b)
                nc.scalar.copy(x_t[0], xn_all[:, bass.ds(b * T, T)]).then_inc(s_xhi, 1)
                if not first:
                    high_part(b - 1, N_BLK - 1)
                block_silu(b, first, 0)
                block_silu(b, first, 1)
                high_part(b, 0)
                wait(act, s_ct, b + 1)
                wait(act, s_bc, b * N_MOE)
                nc.scalar.copy(comb_t[0:2 * EXPERTS, :], banks[0:2 * EXPERTS, CT, :]).then_inc(s_ctr, 1)
                high_part(b, 1)
                if not first:
                    silu_of_sum(b - 1)
                wait(act, s_gp, b + 1)
                wait(act, s_yg, b)
                nc.scalar.activation(gated, banks[:, G, :], ACT.Silu, bias=vec[:, 3:4]).then_inc(s_gs, 1)
                block_silu(b, first, 2)
                wait(act, s_ytr, b + 1)
                nc.scalar.activation(y_t, banks[:, YT, :], ACT.Identity, bias=vec[:, 2:3], scale=vec[:, 1:2]).then_inc(s_yt, 1)
                for k in range(3, N_BLK):
                    block_silu(b, first, k)
                    high_part(b, k - 1)

            def end(b):
                high_part(b, N_BLK - 1)
                silu_of_sum(b)

            sequences(act, body, end)

        @block.vector
        def _(dve):
            nc.vector.memset(comb_t.bitcast(F32), 0.0).then_inc(s_zero, 1)
            comb_halves = comb_parts.rearrange("p (j w e) -> p j w e", j=TILES, w=2)
            dve.wait_ge(s_std, 1)

            def multiply(b):
                wait(dve, s_g, b + 1)
                wait(dve, s_tot, b + 1)
                wait(dve, s_bt, b)
                nc.vector.tensor_tensor(product, total, silu_ffn, ALU.mult).then_inc(s_prod, 1)

            def residual(b):
                wait(dve, s_bt, b + 1)
                wait(dve, s_xin, b * 16 + 16)
                wait(dve, s_out, b * 16)
                nc.vector.tensor_tensor(result, banks[:, CT, :], x_in, ALU.add).then_inc(s_res, 1)

            def body(b, first):
                wait(dve, s_xhi, b + 1)
                nc.vector.tensor_tensor(x_t[1], xn_all[:, bass.ds(b * T, T)], x_t[0].bitcast(F32),
                                        ALU.subtract).then_inc(s_xlo, 1)
                comb = comb_all[:, bass.ds(b * (TILES * EXPERTS), TILES * EXPERTS)].rearrange("p (j e) -> p j e", j=TILES)
                wait(dve, s_ct, b)
                nc.vector.tensor_copy(comb_halves[:, :, 0, :].bitcast(F32R), comb).then_inc(s_cp, 1)
                wait(dve, s_cp, 2 * b + 1)
                nc.vector.tensor_tensor(comb_halves[:, :, 1, :].bitcast(F32R), comb, comb_halves[:, :, 0, :],
                                        ALU.subtract).then_inc(s_cp, 1)
                wait(dve, s_yn, b)
                nc.vector.reciprocal(y_rstd, y_std[:, bass.ds(b * (TILES * HEADS), TILES * HEADS)]).then_inc(s_rstd, 1)
                wait(dve, s_rstd, b + 1)
                wait(dve, s_ytr, b)
                nc.vector.tensor_tensor(yn.rearrange("p (h e) -> p h e", e=HD),
                                        y_all[:, bass.ds(b * T, T)].rearrange("p (h e) -> p h e", e=HD),
                                        y_rstd.unsqueeze(2).broadcast_to([P, TILES * HEADS, HD]), ALU.mult).then_inc(s_yn, 1)
                if not first:
                    multiply(b - 1)
                for m in range(N_MOE):
                    k = m + N_SH
                    wait(dve, s_silu, b * N_BLK + k + 1)
                    wait(dve, s_bc, b * N_MOE + m + 1)
                    wait(dve, s_lo, b * N_BLK + k - 1)
                    nc.vector.tensor_tensor(hidden[k % 2], act_out[m % 2], banks[:, B + m % 2, :],
                                            ALU.mult).then_inc(s_h, 1)
                    if m == 2 and not first:
                        residual(b - 1)
                    if m == 6:
                        wait(dve, s_pr, b + 1)
                        wait(dve, s_prod, b)
                        nc.vector.tensor_tensor(total, banks[:, G, :], skip_all[:, bass.ds(b * T, T)],
                                                ALU.add).then_inc(s_tot, 1)

            def end(b):
                multiply(b)
                residual(b)

            sequences(dve, body, end)


def kernel(**inputs):
    import numpy as _np
    import concourse.bacc as _bacc
    from concourse import mybir as _mybir
    from concourse.bass_utils import run_bass_kernel_spmd as _run

    a = {k.replace("L0_", ""): _np.asarray(v) for k, v in inputs.items()}
    C = 128
    qkvff = a["attn_w_qkvff"].T
    swap = _np.arange(C) ^ 1
    q, k = qkvff[:, 0:C], qkvff[:, C:2 * C]
    w_up = _np.concatenate([q, q[:, swap], k, k[:, swap], qkvff[:, 2 * C:], a["attn_w_gated"].T, a["ffn_shared_up"],
                            a["ffn_expert_up"].transpose(1, 0, 2).reshape(C, -1)], 1)
    w_down = _np.concatenate([a["ffn_expert_down"].reshape(-1, C), a["ffn_shared_down"], a["attn_w_ff"].T,
                              a["attn_w_proj"].T], 0).reshape(-1, C, C).transpose(1, 0, 2).reshape(C, -1)
    vecs = _np.stack([a["attn_rms_w"], a["attn_gn_w"], a["attn_gn_b"], a["attn_b_gated"], a["attn_b_proj"]], 1)
    x = a["attn_x"]
    arrays = {"x": x.reshape(-1, C), "w_up": w_up, "w_down": w_down, "w_gate": a["ffn_gate_weight"].T, "vecs": vecs}
    arrays.update(shape_tables())
    arrays = {k: _np.ascontiguousarray(v) for k, v in arrays.items()}

    nc = _bacc.Bacc("TRN2", target_bir_lowering=False, num_devices=1)
    args = [nc.dram_tensor(k, v.shape, _mybir.dt.from_np(v.dtype), kind="ExternalInput").ap() for k, v in arrays.items()]
    out = nc.dram_tensor("out", arrays["x"].shape, _mybir.dt.from_np(_np.dtype("float32")), kind="ExternalOutput").ap()
    build(nc, *args, out)
    r = _run(nc, [arrays], core_ids=[0])
    return r.results[0]["out"].reshape(x.shape)
```

```python
from contextlib import ExitStack

import numpy as np

import concourse.bass as bass
from concourse import mybir

P = 128
ALU = mybir.AluOpType
ACT = mybir.ActivationFunctionType
AX = mybir.AxisListType.X
F32 = mybir.dt.float32
F32R = mybir.dt.float32r
F16 = mybir.dt.float16
I32 = mybir.dt.int32

HEADS = 16
HD = 8
GROUPS = 4
CHUNK = 32
T = 512
CHUNKS = T // CHUNK
TILES = T // P
LN_EPS = 1e-5
GN_EPS = 1e-5
EXPERTS = 16
TOP_K = 4
TOPK_GROUP = 2
N_GROUP = 4
ROUTED_SCALING = 2.5

Q, K, V, FF, GATED, SHARED, MOE = 0, 1, 2, 3, 5, 6, 8
N_UP = 16
RMS_BLOCKS = 5
D_MOE, D_SHARED, D_FF, D_PROJ = 0, 8, 10, 12
N_DOWN = 13
N_SPLIT = 10
FF_DOWN = RMS_BLOCKS
N_EARLY = RMS_BLOCKS + D_PROJ - D_FF
N_LATE = N_UP + N_DOWN - N_EARLY
SCRATCH = 15
XPARTS = 4
PARTS = ((0, 0), (0, 1), (1, 0))
PAIRS_SWAPPED = [i ^ 1 for i in range(32)]
ROUTE_STEPS = 15
FILLER, MARK = -1.0, -3.0


def shape_tables():
    C = P
    t = np.arange(T, dtype=np.float64)
    ch = np.arange(C)
    scale_vec = (np.arange(0, C, 2) + 0.4 * C) / (1.4 * C)
    inv_freq = 1.0 / 10000.0 ** (np.arange(C // 2) / (C // 2))
    angle = t[None, :] * inv_freq[ch // 2][:, None]
    sign = np.where(ch % 2 == 0, -1.0, 1.0)[:, None]
    gamma = 1.0 - 2.0 ** (-5.0 - ch // HD)
    local = np.arange(T) % CHUNK
    base = gamma * scale_vec[ch // 2] ** (1 / 64.0)
    grow = base[:, None] ** (local[None, :] + 1.0)
    cos, sin = np.cos(angle), np.sin(angle) * sign
    rope = np.stack([cos * grow * HD ** -0.5, sin * grow * HD ** -0.5, cos / grow, sin / grow], 1)
    in_group = (ch // HD) % 4
    decay = base ** CHUNK
    col = np.arange(32)
    same_head = in_group[:, None] == (col // HD)[None, :]
    state_mask = same_head * decay[:, None]
    carry = np.repeat(np.repeat(decay[:, None], 32, 1)[:, :, None], CHUNKS, 2)
    carry[:, :, 0] = 0.0
    causal = (ch % CHUNK)[:, None] <= np.arange(CHUNK)[None, :]
    head_of = in_group[:, None] == np.arange(4)[None, :]
    router = np.zeros((P, 8, P))
    for m in range(8):
        for half in range(2):
            for part in range(2):
                router[16 * part + 2 * m + half, m, 64 * half:64 * half + 64] = 1.0
    out = {
        "t_rope": rope.reshape(C, 4 * T), "t_state": state_mask,
        "t_carry": carry.reshape(C, T), "t_causal": causal, "t_head": head_of,
        "t_router": router.reshape(P, 8 * P), "t_ident": np.eye(P),
    }
    return {k: np.ascontiguousarray(v, dtype=np.float32) for k, v in out.items()}


def wait(engine, semaphore, value):
    if not isinstance(value, int) or value > 0:
        engine.wait_ge(semaphore, value)


class Shared:
    pass


def build(nc, x, w_up, w_down, w_gate, vecs, t_rope, t_state, t_carry, t_causal, t_head,
          t_router, t_ident, out):
    rows = x.shape[0]
    NB = rows // T
    NT = rows // P
    g = Shared()
    with ExitStack() as ctx, ExitStack() as early:
        def sb(name, shape, dt=F32):
            return ctx.enter_context(nc.sbuf_tensor(name, shape, dt))

        def sb_early(name, shape, dt=F32):
            return early.enter_context(nc.sbuf_tensor(name, shape, dt))

        def sem(name):
            return ctx.enter_context(nc.semaphore(name))

        g.NB, g.NT = NB, NT
        g.late_raw = late_raw = sb("late_raw", [P, N_LATE * P])
        g.vec = vec = sb("vec", [P, 5])
        g.ident = ident = sb("ident", [P, P])
        g.eps = eps = sb("eps", [P, 1])
        g.xn_all = xn_all = sb("xn_all", [P, rows])
        g.y_all = y_all = sb("y_all", [P, rows])
        g.skip_all = skip_all = sb("skip_all", [P, rows])
        g.comb_all = sb("comb_all", [P, NT * EXPERTS])
        g.y_var = sb("y_var", [P, NT * HEADS])
        g.early_w = early_w = [sb_early("early_w_hi", [P, N_EARLY * P], F32R), sb_early("early_w_lo", [P, N_EARLY * P], F32R)]
        g.gate_w = sb_early("gate_w", [P, EXPERTS])
        g.rope = rope = sb_early("rope", [P, 4, T])
        g.state_mask = state_mask = sb_early("state_mask", [P, 32])
        g.carry = carry = sb_early("carry", [P, T])
        g.causal = causal = sb_early("causal", [P, CHUNK])
        g.head_of = head_of = sb_early("head_of", [P, 4])
        g.row_mean = row_mean = sb_early("row_mean", [P, NT])
        g.row_rstd = row_rstd = sb_early("row_rstd", [P, NT])
        g.row_rms = row_rms = sb_early("row_rms", [P, NT])
        g.vexp = vexp = sb_early("vexp", [P, CHUNKS * P])
        scratch = sb_early("scratch", [P, SCRATCH * T])

        g.banks = ctx.enter_context(nc.psum_tensor("banks", [P, 8, T], F32))
        g.scratch = scratch
        g.x_rows = x_rows = x.rearrange("(n p) c -> p n c", p=P)
        g.out_rows = out.rearrange("(n p) c -> p n c", p=P)
        seqs = xn_all[:, :].rearrange("p (n c) -> p n c", c=P)

        s_x = [sem(f"x_loaded{i}") for i in range(XPARTS)]
        s_raw = sem("early_weights_loaded")
        g.s_late = s_late = sem("late_weights_loaded")
        g.s_weights = s_weights = sem("weights_loaded")
        g.s_tables = s_tables = sem("tables_loaded")
        s_ctab = sem("causal_loaded")
        g.s_rope = s_rope = sem("rope_loaded")
        s_bn = sem("bn_done")
        s_step = sem("p_step")
        s_var = sem("variances_ready")
        s_std = sem("deviations_ready")
        s_rms_fold = sem("rms_folded")
        s_amax, s_amax_all = sem("largest_of_partition"), sem("largest_of_all")
        s_fold = sem("v_centred")
        s_inverse, s_scaled = sem("scales_ready"), sem("q_k_scaled")
        s_hi = sem("high_parts")
        g.s_split = s_split = sem("weights_split")
        s_tab_scaled = sem("tables_scaled")
        g.s_zero = s_zero = sem("vexp_zeroed")

        early_raw = skip_all[:, 0:N_EARLY * P]
        g.t_router = t_router

        bn = scratch[:, 0:NT * 6]
        small = scratch[:, NT * 6:NT * 6 + 8 * NT]
        two_var = small[:, 0:2 * NT]
        two_std = small[:, 2 * NT:4 * NT]
        mean_sum, mean_gap, nrm = (small[:, i * NT:(i + 1) * NT] for i in (4, 5, 6))
        v_mean = small[:, 7 * NT:7 * NT + HEADS]
        spare = small[:, 7 * NT + HEADS:8 * NT]
        amax, power, inverse, both = spare[:, 0:2], spare[:, 2:4], spare[:, 4:6], spare[:, 6:7]
        amax_all, amin = spare[:, 8:10], spare[:, 10:12]

        with nc.Block() as block:
            @block.sync
            def _(sp):
                n = NT // XPARTS
                for i in range(XPARTS):
                    sp.dma_start(seqs[:, i * n:(i + 1) * n, :], x_rows[:, i * n:(i + 1) * n, :]).then_inc(s_x[i], 16)
                n_first = (N_UP - RMS_BLOCKS) * P
                sp.dma_start(late_raw[:, 0:n_first], w_up[:, RMS_BLOCKS * P:]).then_inc(s_late, 16)
                sp.dma_start(late_raw[:, n_first:n_first + N_SPLIT * P], w_down[:, 0:N_SPLIT * P]).then_inc(s_late, 16)
                sp.dma_start(late_raw[:, n_first + N_SPLIT * P:], w_down[:, D_PROJ * P:]).then_inc(s_late, 16)
                sp.dma_start(g.gate_w[:], w_gate).then_inc(s_weights, 16)

            @block.scalar
            def _(act):
                act.dma_start(vec[:], vecs).then_inc(s_raw, 16)
                act.dma_start(early_raw[:, 0:RMS_BLOCKS * P], w_up[:, 0:RMS_BLOCKS * P]).then_inc(s_raw, 16)
                act.dma_start(early_raw[:, RMS_BLOCKS * P:], w_down[:, D_FF * P:D_PROJ * P]).then_inc(s_raw, 16)
                act.dma_start(rope[:, :, :], t_rope.rearrange("p (n t) -> p n t", n=4)).then_inc(s_rope, 16)
                act.wait_ge(s_raw, 48)
                nc.scalar.activation(early_raw[:, 0:RMS_BLOCKS * P], early_raw[:, 0:RMS_BLOCKS * P], ACT.Copy,
                                     scale=vec[:, 0:1]).then_inc(s_rms_fold, 1)
                act.wait_ge(s_inverse, 1)
                act.wait_ge(s_amax, 1)
                nc.scalar.activation(early_raw[:, Q * P:K * P], early_raw[:, Q * P:K * P], ACT.Copy,
                                     scale=inverse[:, 0:1]).then_inc(s_scaled, 1)
                nc.scalar.activation(early_raw[:, K * P:V * P], early_raw[:, K * P:V * P], ACT.Copy,
                                     scale=inverse[:, 1:2]).then_inc(s_scaled, 1)
                act.wait_ge(s_scaled, 2)
                act.wait_ge(s_fold, 1)
                nc.scalar.copy(early_w[0][:, :], early_raw).then_inc(s_hi, 1)
                act.wait_ge(s_var, 2)
                nc.scalar.activation(two_std, two_var, ACT.Sqrt).then_inc(s_std, 1)

            @block.gpsimd
            def _(pool):
                pool.dma_start(causal[:], t_causal).then_inc(s_ctab, 16)
                pool.dma_start(state_mask[:], t_state).then_inc(s_ctab, 16)
                pool.dma_start(carry[:], t_carry).then_inc(s_tables, 16)
                pool.dma_start(head_of[:], t_head).then_inc(s_tables, 16)
                pool.dma_start(ident[:], t_ident).then_inc(s_tables, 16)
                nc.gpsimd.memset(vexp[:, :], 0.0).then_inc(s_zero, 1)
                pool.wait_ge(s_amax, 1)
                nc.gpsimd.partition_all_reduce(amax_all, amax, P, bass.bass_isa.ReduceOp.max).then_inc(s_amax_all, 1)
                pool.wait_ge(s_hi, 1)
                nc.gpsimd.tensor_tensor(early_w[1][:, :], early_raw, early_w[0][:, :].bitcast(F32),
                                        ALU.subtract).then_inc(s_split, 1)

            @block.vector
            def _(dve):
                steps = [0]

                def step(instruction):
                    instruction.then_inc(s_step, 1)
                    steps[0] += 1
                    dve.wait_ge(s_step, steps[0])

                def statistics(i):
                    dve.wait_ge(s_x[i], 16)
                    per = NT // XPARTS // 8
                    with dve.Fori(i * per, (i + 1) * per) as n:
                        for j in range(8):
                            nc.vector.bn_stats(bn[:, bass.ds(n * 48 + j * 6, 6)],
                                               xn_all[:, bass.ds(n * 8 * P + j * P, P)]).then_inc(s_bn, 1)

                nc.vector.memset(eps[:, :], GN_EPS)
                statistics(0)
                statistics(1)
                dve.wait_ge(s_rms_fold, 1)
                qk_w = early_raw[:, Q * P:V * P].rearrange("p (a c) -> p a c", a=2)
                nc.vector.tensor_reduce(amax, qk_w, AX, ALU.max).then_inc(s_step, 1)
                steps[0] += 1
                step(nc.vector.tensor_reduce(amin, qk_w, AX, ALU.min))
                nc.vector.scalar_tensor_tensor(amax, amin, -1.0, amax, ALU.mult, ALU.max).then_inc(s_amax, 1)
                v_w = early_raw[:, V * P:(V + 1) * P].rearrange("p (h d) -> p h d", d=HD)
                step(nc.vector.tensor_reduce(v_mean, v_w, AX, ALU.add))
                step(nc.vector.tensor_scalar(v_mean, v_mean, 1.0 / HD, None, ALU.mult))
                nc.vector.tensor_tensor(v_w, v_w, v_mean.unsqueeze(2).broadcast_to([P, HEADS, HD]),
                                        ALU.subtract).then_inc(s_fold, 1)
                statistics(2)
                dve.wait_ge(s_amax_all, 1)
                step(nc.vector.tensor_scalar(power, amax_all, 2.0 ** -60, None, ALU.max))
                step(nc.vector.tensor_scalar(power.bitcast(I32), power.bitcast(I32), 0x7F800000, None, ALU.bitwise_and))
                nc.vector.reciprocal(inverse, power).then_inc(s_inverse, 1)
                nc.vector.tensor_tensor(both, power[:, 0:1], power[:, 1:2], ALU.mult).then_inc(s_step, 1)
                steps[0] += 1
                dve.wait_ge(s_ctab, 32)
                dve.wait_ge(s_step, steps[0])
                nc.vector.tensor_scalar(causal[:, :], causal[:, :], both, None, ALU.mult).then_inc(s_tab_scaled, 1)
                nc.vector.tensor_scalar(state_mask[:, :], state_mask[:, :], both, None, ALU.mult).then_inc(s_tab_scaled, 1)
                statistics(3)
                dve.wait_ge(s_bn, NT)
                b = bn.rearrange("p (n s) -> p n s", s=6)
                var, var_eps = two_var[:, NT:2 * NT], two_var[:, 0:NT]
                nc.vector.tensor_tensor(mean_sum, b[:, :, 1], b[:, :, 4], ALU.add).then_inc(s_step, 1)
                nc.vector.tensor_tensor(mean_gap, b[:, :, 1], b[:, :, 4], ALU.subtract).then_inc(s_step, 1)
                steps[0] += 2
                step(nc.vector.tensor_tensor(var_eps, b[:, :, 2], b[:, :, 5], ALU.add))
                nc.vector.tensor_scalar(row_mean[:, :], mean_sum, 0.5, None, ALU.mult).then_inc(s_step, 1)
                steps[0] += 1
                step(nc.vector.scalar_tensor_tensor(mean_gap, mean_gap, 0.25, mean_gap, ALU.mult, ALU.mult))
                nc.vector.scalar_tensor_tensor(var, var_eps, 1.0 / P, mean_gap, ALU.mult, ALU.add).then_inc(s_var, 1)
                dve.wait_ge(s_var, 1)
                nc.vector.tensor_scalar(var_eps, var, LN_EPS, None, ALU.add).then_inc(s_var, 1)
                dve.wait_ge(s_std, 1)
                step(nc.vector.reciprocal(row_rstd[:, :], two_std[:, 0:NT]))
                step(nc.vector.tensor_tensor(nrm, two_std[:, NT:2 * NT], row_rstd[:, :], ALU.mult))
                step(nc.vector.tensor_scalar(nrm, nrm, 1e-8, None, ALU.max))
                step(nc.vector.reciprocal(row_rms[:, :], nrm))
                dve.wait_ge(s_tab_scaled, 2)

        attend(nc, sem, g)
        early.close()
        combine(nc, sem, g)


def attend(nc, sem, g):
    with ExitStack() as ctx:
        attend_in(nc, sem, g, lambda name, shape, dt=F32: ctx.enter_context(nc.sbuf_tensor(name, shape, dt)))


def attend_in(nc, sem, g, sb):
    NB, banks, early_w = g.NB, g.banks, g.early_w
    xn_all, y_all, skip_all, comb_all, y_var = g.xn_all, g.y_all, g.skip_all, g.comb_all, g.y_var
    ident, rope, vec, vexp = g.ident, g.rope, g.vec, g.vexp

    def part(at, count=1):
        return g.scratch[:, at * T:(at + count) * T]

    xn, xn_t = part(0), part(1)
    ff = [part(2), part(3)]
    cosine, sine = part(4), part(5)
    q_t, k_t = part(6), part(7)
    k_rows, v_rows = part(8), part(9)
    probs = part(10, 4)
    u_in = xs = y_sq = part(14)
    states = sb("states", [P, T])[:, :]
    xs_t = [sb("xs_t_hi", [P, T], F32R)[:, :], sb("xs_t_lo", [P, T], F32R)[:, :]]
    ff_hi = [sb(f"ff_hi{k}", [P, T], F32R)[:, :] for k in range(2)]
    ff_lo = [sb(f"ff_lo{k}", [P, T], F32R)[:, :] for k in range(2)]
    q_16 = sb("q_16", [P, 2, T], F16)
    k_16 = sb("k_16", [P, 2, T], F16)
    k_heads = sb("k_heads", [P, 2, 4 * T], F16)
    SLOTS = EXPERTS + 4
    score = sb("score", [P, TILES * EXPERTS])[:, :]
    pairs = sb("pairs", [P, TILES * N_GROUP, 6])
    sums = sb("sums", [P, TILES, N_GROUP + 6])
    group_marked = sb("group_marked", [P, TILES, N_GROUP + 6])
    small = sb("small", [P, 3, TILES])
    kept = sb("kept", [P, TILES, SLOTS])
    marked = sb("marked", [P, TILES, SLOTS])
    largest = sb("largest", [P, TILES, 8])

    s_norm = sem("a_rows_normed")
    s_norm_s = sem("a_rows_rms_normed")
    s_tr_s = sem("a_xs_transposed")
    s_tr = sem("a_xn_transposed")
    s_xnt = sem("a_xn_t_ready")
    s_xst = sem("a_xs_t_ready")
    s_keep = sem("a_xn_t_kept")
    s_gate = sem("a_logits_ready")
    s_score = sem("a_gate_scores_ready")
    s_route = sem("a_route_step")
    s_filled = sem("a_fillers_set")
    s_ffup = sem("a_ff_up_done")
    s_gelu = sem("a_gelu_ready")
    s_ff_hi = sem("a_ff_high_part")
    s_ff_lo = sem("a_ff_low_part")
    s_ffdn = sem("a_ff_down_done")
    s_skip = sem("a_skip_kept")
    s_kp = sem("a_k_projected")
    s_kr = sem("a_k_read")
    s_ks = sem("a_k_sine_products")
    s_kt = sem("a_k_t_ready")
    s_kp16 = sem("a_k_high_part")
    s_kl16 = sem("a_k_low_part")
    s_kh = sem("a_k_heads_ready")
    s_qp = sem("a_q_projected")
    s_qr = sem("a_q_read")
    s_qs = sem("a_q_sine_products")
    s_qt = sem("a_q_t_ready")
    s_qp16 = sem("a_q_high_part")
    s_ql16 = sem("a_q_low_part")
    s_vp = sem("a_v_projected")
    s_vr = sem("a_v_rows_ready")
    s_vx = sem("a_v_expanded")
    s_ktr = sem("a_k_transposed")
    s_krow = sem("a_k_rows_ready")
    s_u = sem("a_updates_done")
    s_um = sem("a_updates_masked")
    s_st = sem("a_states_ready")
    s_sc = sem("a_scores_done")
    s_p = sem("a_probs_ready")
    s_y = sem("a_y_done")
    s_yk = sem("a_y_kept")
    s_ysq = sem("a_y_squared")
    s_yv = sem("a_y_variances")
    s_split, s_weights, s_tables, s_zero = g.s_split, g.s_weights, g.s_tables, g.s_zero

    def split_matmul(out, block, rhs, first=True, final=True):
        for i, (a, c) in enumerate(PARTS):
            last = nc.tensor.matmul(out, early_w[a][:, block * P:(block + 1) * P], rhs[c],
                                    start=first and i == 0, stop=final and i == 2)
        return last

    with nc.Block() as block:
        @block.sync
        def _(sp):
            with sp.Fori(0, NB) as b:
                wait(sp, s_xnt, b + 1)
                wait(sp, s_norm, b + 1)
                sp.dma_start(xn_all[:, bass.ds(b * T, T)], xn_t).then_inc(s_keep, 16)
            sp.wait_ge(s_keep, 16 * NB)

        @block.tensor
        def _(pe):
            pe.wait_ge(s_split, 1)
            pe.wait_ge(s_weights, 16)
            pe.wait_ge(s_tables, 48)

            def transposes(b):
                wait(pe, s_norm_s, b + 1)
                wait(pe, s_qr, 2 * b)
                for j in range(TILES):
                    last = nc.tensor.transpose(banks[:, 5, j * P:(j + 1) * P], xs[:, j * P:(j + 1) * P], ident[:, :])
                last.then_inc(s_tr_s, 1)
                for j in range(TILES):
                    last = nc.tensor.transpose(banks[:, 4, j * P:(j + 1) * P], xn[:, j * P:(j + 1) * P], ident[:, :])
                last.then_inc(s_tr, 1)

            def feed_forward_up(b, k):
                wait(pe, s_xst, 2 * b + 2)
                wait(pe, s_krow, b)
                wait(pe, s_vr, b)
                split_matmul(banks[:, 6 + k, :], FF + k, xs_t).then_inc(s_ffup, 1)

            def project_k(b):
                wait(pe, s_xnt, b + 1)
                split_matmul(banks[:, 4, :], K, xs_t).then_inc(s_kp, 1)

            def feed_forward_down(b, k):
                wait(pe, s_ff_lo, 2 * b + k + 1)
                last = split_matmul(banks[:, 6, :], FF_DOWN + k, (ff_hi[k], ff_lo[k]), k == 0, k == 1)
                last.then_inc(s_ffdn, 1)

            def gate(b):
                wait(pe, s_gelu, 2 * b + 2)
                for j in range(TILES):
                    last = nc.tensor.matmul(banks[:, 7, j * EXPERTS:(j + 1) * EXPERTS], xn_t[:, j * P:(j + 1) * P],
                                            g.gate_w[:, :], start=True, stop=True)
                last.then_inc(s_gate, 1)

            def project_q(b):
                wait(pe, s_kr, 2 * b + 2)
                split_matmul(banks[:, 4, :], Q, xs_t).then_inc(s_qp, 1)

            def project_v(b):
                wait(pe, s_score, b + 1)
                for j in range(TILES):
                    for i, (a, c) in enumerate(PARTS):
                        last = nc.tensor.matmul(banks[:, 7, j * P:(j + 1) * P], xs_t[a][:, j * P:(j + 1) * P],
                                                early_w[c][:, V * P:(V + 1) * P], start=i == 0, stop=i == 2)
                last.then_inc(s_vp, 1)

            def k_by_rows(b):
                wait(pe, s_kt, b + 1)
                wait(pe, s_skip, b + 1)
                for j in range(TILES):
                    last = nc.tensor.transpose(banks[:, 6, j * P:(j + 1) * P], k_t[:, j * P:(j + 1) * P], ident[:, :])
                last.then_inc(s_ktr, 1)

            def wait_for_state_updates(b):
                wait(pe, s_krow, b + 1)
                wait(pe, s_vr, b + 1)
                wait(pe, s_yk, b)

            def state_updates(b):
                for j in range(TILES):
                    for c in range(4):
                        for h in range(GROUPS):
                            rows = slice(32 * c, 32 * c + 32)
                            cols = slice(j * P + 32 * h, j * P + 32 * h + 32)
                            last = nc.tensor.matmul(banks[32 * h:32 * h + 32, c, 32 * j:32 * j + 32],
                                                    k_rows[rows, cols], v_rows[rows, cols], start=True, stop=True)
                return last

            def scores(b):
                wait(pe, s_kh, b + 1)
                wait(pe, s_qp16, b + 1)
                wait(pe, s_ql16, b + 1)
                wait(pe, s_um, b + 1)
                for h in range(GROUPS):
                    for n in range(CHUNKS):
                        rows, cols = slice(32 * h, 32 * h + 32), slice(CHUNK * n, CHUNK * n + CHUNK)
                        for i, (a, c) in enumerate(PARTS):
                            last = nc.tensor.matmul(banks[:, h, cols], k_heads[rows, a, n * P:(n + 1) * P],
                                                    q_16[rows, c, cols], start=i == 0, stop=i == 2)
                    last.then_inc(s_sc, 1)

            def outputs_of_chunks(b, groups):
                wait(pe, s_st, b + 1)
                wait(pe, s_vx, b + 1)
                for h in groups:
                    wait(pe, s_p, 4 * b + h + 1)
                    for n in range(CHUNKS):
                        j, c = n // 4, n % 4
                        nc.tensor.matmul(banks[32 * c:32 * c + 32, h, 32 * j:32 * j + 32],
                                         probs[:, h * T + CHUNK * n:h * T + CHUNK * n + CHUNK],
                                         vexp[:, n * P + 32 * h:n * P + 32 * h + 32],
                                         start=j == 0, stop=n == 0, skip_group_check=True)

            def outputs_of_states(b, groups):
                st = states.rearrange("p (e n) -> p e n", n=CHUNKS)
                for n in range(1, CHUNKS):
                    j, c = n // 4, n % 4
                    for h in groups:
                        rows = slice(32 * h, 32 * h + 32)
                        last = nc.tensor.matmul(banks[32 * c:32 * c + 32, h, 32 * j:32 * j + 32],
                                                q_t[rows, CHUNK * n:CHUNK * n + CHUNK], st[rows, :, n - 1],
                                                start=False, stop=True, skip_group_check=True)
                return last

            transposes(0)
            feed_forward_up(0, 0)
            feed_forward_up(0, 1)
            project_k(0)
            gate(0)
            feed_forward_down(0, 0)
            feed_forward_down(0, 1)
            project_q(0)
            project_v(0)
            k_by_rows(0)
            transposes(1)

            def body(b, last=False):
                feed_forward_up(b + 1, 0)
                wait_for_state_updates(b)
                feed_forward_up(b + 1, 1)
                project_k(b + 1)
                state_updates(b).then_inc(s_u, 1)
                gate(b + 1)
                scores(b)
                feed_forward_down(b + 1, 0)
                feed_forward_down(b + 1, 1)
                project_q(b + 1)
                outputs_of_chunks(b, (0, 1))
                project_v(b + 1)
                outputs_of_states(b, (0, 1))
                k_by_rows(b + 1)
                outputs_of_chunks(b, (2, 3))
                if not last:
                    transposes(b + 2)
                outputs_of_states(b, (2, 3)).then_inc(s_y, 1)

            body(0)
            with pe.Fori(1, NB - 2) as b:
                body(b)
            body(NB - 2, True)
            wait_for_state_updates(NB - 1)
            pe.wait_ge(s_qr, 2 * NB)
            nc.tensor.transpose(banks[:, 5, 0:P], xn[:, 0:P], ident[:, :])
            state_updates(NB - 1).then_inc(s_u, 1)
            scores(NB - 1)
            outputs_of_chunks(NB - 1, range(GROUPS))
            outputs_of_states(NB - 1, range(GROUPS)).then_inc(s_y, 1)

        @block.scalar
        def _(act):
            vx = vexp[:, :].rearrange("p (j c g h e) -> p j c g h e", j=TILES, c=4, g=GROUPS, h=4)
            vr = v_rows.rearrange("p (j g h e) -> p j g h e", j=TILES, g=GROUPS, h=4)

            def norm_s(b):
                wait(act, s_norm, b + 1)
                wait(act, s_tr, b)
                wait(act, s_st, b - 1)
                for j in range(TILES):
                    last = nc.scalar.activation(xs[:, j * P:(j + 1) * P], xn[:, j * P:(j + 1) * P], ACT.Copy,
                                                scale=g.row_rms[:, bass.ds(b * TILES + j, 1)])
                last.then_inc(s_norm_s, 1)

            def x_by_channels(b):
                wait(act, s_tr_s, b + 1)
                wait(act, s_vp, b)
                nc.scalar.copy(xs_t[0], banks[:, 5, :]).then_inc(s_xst, 1)
                wait(act, s_tr, b + 1)
                wait(act, s_keep, b * 16)
                wait(act, s_gate, b)
                wait(act, s_skip, b)
                nc.scalar.copy(xn_t, banks[:, 4, :]).then_inc(s_xnt, 1)

            def gelu(b):
                wait(act, s_ffdn, 2 * b)
                for k in range(2):
                    wait(act, s_ffup, 2 * b + k + 1)
                    nc.scalar.activation(ff[k], banks[:, 6 + k, :], ACT.Gelu).then_inc(s_gelu, 1)
                for k in range(2):
                    wait(act, s_gelu, 2 * b + k + 1)
                    nc.scalar.copy(ff_hi[k], ff[k]).then_inc(s_ff_hi, 1)

            def gate_scores(b):
                wait(act, s_gate, b + 1)
                wait(act, s_route, b * ROUTE_STEPS)
                nc.scalar.activation(score, banks[:, 7, 0:TILES * EXPERTS], ACT.Sigmoid).then_inc(s_score, 1)

            def high_part_k(b):
                wait(act, s_kt, b + 1)
                wait(act, s_kh, b)
                nc.scalar.copy(k_16[:, 0, :], k_t).then_inc(s_kp16, 1)

            def high_part_q(b):
                wait(act, s_qt, b + 1)
                wait(act, s_sc, 4 * b)
                nc.scalar.copy(q_16[:, 0, :], q_t).then_inc(s_qp16, 1)

            def rows_of_v(b):
                wait(act, s_vp, b + 1)
                wait(act, s_u, b)
                nc.scalar.copy(v_rows, banks[:, 7, :]).then_inc(s_vr, 1)

            def rows_of_k(b):
                wait(act, s_ktr, b + 1)
                wait(act, s_u, b)
                nc.scalar.copy(k_rows, banks[:, 6, :]).then_inc(s_krow, 1)

            def expand_v(b):
                wait(act, s_vr, b + 1)
                wait(act, s_y, b)
                for h in range(4):
                    for c in range(4):
                        last = nc.scalar.copy(vx[32 * h:32 * h + 32, :, c, :, h, :], vr[32 * c:32 * c + 32, :, :, h, :])
                last.then_inc(s_vx, 1)

            def keep_y(b):
                wait(act, s_y, b + 1)
                nc.scalar.copy(y_all[:, bass.ds(b * T, T)].rearrange("p (j g e) -> p j g e", j=TILES, g=GROUPS),
                               banks[:, 0:4, 0:P].rearrange("p g (j e) -> p j g e", j=TILES)).then_inc(s_yk, 1)

            def wait_for_square(b, last=False):
                wait(act, s_yk, b + 1)
                wait(act, s_tr, NB if last else b + 3)

            def square_y(b):
                nc.scalar.activation(y_sq, y_all[:, bass.ds(b * T, T)], ACT.Square).then_inc(s_ysq, 1)

            def deviations(cols, count):
                act.wait_ge(s_yv, count)
                nc.scalar.activation(y_var[:, cols], y_var[:, cols], ACT.Sqrt, bias=g.eps[:, 0:1], scale=1.0 / HD)

            act.wait_ge(s_zero, 1)
            norm_s(0)
            x_by_channels(0)
            gelu(0)
            gate_scores(0)
            high_part_k(0)
            norm_s(1)
            rows_of_v(0)
            rows_of_k(0)
            x_by_channels(1)
            high_part_q(0)

            def body(b, last=False):
                gelu(b + 1)
                expand_v(b)
                gate_scores(b + 1)
                high_part_k(b + 1)
                if not last:
                    norm_s(b + 2)
                rows_of_v(b + 1)
                if not last:
                    x_by_channels(b + 2)
                rows_of_k(b + 1)
                keep_y(b)
                wait_for_square(b, last)
                high_part_q(b + 1)
                square_y(b)

            body(0)
            with act.Fori(1, NB - 2) as b:
                body(b)
            body(NB - 2, True)
            expand_v(NB - 1)
            deviations(slice(0, (NB - 1) * TILES * HEADS), NB - 1)
            keep_y(NB - 1)
            wait_for_square(NB - 1, True)
            square_y(NB - 1)
            deviations(slice((NB - 1) * TILES * HEADS, NB * TILES * HEADS), NB)

        @block.vector
        def _(dve):
            row_mean, row_rstd = g.row_mean, g.row_rstd

            def norm_rows(b):
                wait(dve, s_tr, b)
                for j in range(TILES):
                    tile = xn_all[:, bass.ds(b * T + j * P, P)]
                    mean = row_mean[:, bass.ds(b * TILES + j, 1)]
                    last = nc.vector.tensor_scalar(xn[:, j * P:(j + 1) * P], tile, mean,
                                                   row_rstd[:, bass.ds(b * TILES + j, 1)], ALU.subtract, ALU.mult)
                last.then_inc(s_norm, 1)

            def split_x(b):
                wait(dve, s_xst, 2 * b + 1)
                nc.vector.tensor_tensor(xs_t[1], banks[:, 5, :], xs_t[0].bitcast(F32), ALU.subtract).then_inc(s_xst, 1)

            def rotate(b, s_projected, s_rotated, s_ready, at):
                wait(dve, s_projected, b + 1)
                if at == 0:
                    wait(dve, s_kt, b + 1)
                else:
                    wait(dve, s_qt, b)
                nc.vector.tensor_tensor(cosine, banks[:, 4, :], rope[:, at, :], ALU.mult).then_inc(s_rotated, 1)
                nc.vector.stream_shuffle(sine, banks[:, 4, :], PAIRS_SWAPPED).then_inc(s_rotated, 1)
                wait(dve, s_rotated, 2 * b + 2)
                nc.vector.tensor_tensor(sine, sine, rope[:, at + 1, :], ALU.mult).then_inc(s_ready, 1)

            def expand_k(b):
                wait(dve, s_kp16, b + 1)
                wait(dve, s_kl16, b + 1)
                wait(dve, s_sc, 4 * b)
                heads = k_heads[:, :, :].rearrange("p w (n h s) -> p (w n) h s", h=4, s=CHUNK)
                k_chunks = k_16[:, :, :].rearrange("p w (n s) -> p (w n) s", s=CHUNK)
                for h in range(4):
                    last = nc.vector.tensor_scalar(heads[:, :, h, :], k_chunks, g.head_of[:, h:h + 1], None, ALU.mult)
                last.then_inc(s_kh, 1)

            def keep_skip(b):
                wait(dve, s_ffdn, 2 * b + 2)
                wait(dve, s_xnt, b + 1)
                nc.vector.scalar_tensor_tensor(skip_all[:, bass.ds(b * T, T)], banks[:, 6, :], vec[:, 4:5], xn_t,
                                               ALU.add, ALU.add).then_inc(s_skip, 1)

            def carry_states(b):
                wait(dve, s_u, b + 1)
                wait(dve, s_st, b)
                wait(dve, s_yv, b)
                nc.vector.tensor_tensor(u_in.rearrange("p (e j c) -> p j c e", e=32, j=TILES),
                                        banks[:, 0:4, 0:P].rearrange("p c (j e) -> p j c e", j=TILES),
                                        g.state_mask[:, :].unsqueeze(1).unsqueeze(1).broadcast_to([P, TILES, 4, 32]),
                                        ALU.mult).then_inc(s_um, 1)
                wait(dve, s_um, b + 1)
                wait(dve, s_y, b)
                nc.vector.tensor_tensor_scan(states, g.carry[:, :], u_in, 0.0, ALU.mult, ALU.add).then_inc(s_st, 1)

            def mask_scores(b, groups):
                for h in groups:
                    wait(dve, s_sc, 4 * b + h + 1)
                    wait(dve, s_y, b)
                    nc.vector.tensor_tensor(probs[:, h * T:(h + 1) * T].rearrange("p (n t) -> p n t", t=CHUNK),
                                            banks[:, h, :].rearrange("p (n t) -> p n t", t=CHUNK),
                                            g.causal[:, :].unsqueeze(1).broadcast_to([P, CHUNKS, CHUNK]),
                                            ALU.mult).then_inc(s_p, 1)

            def variances(b):
                wait(dve, s_ysq, b + 1)
                nc.vector.tensor_reduce(y_var[:, bass.ds(b * (TILES * HEADS), TILES * HEADS)],
                                        y_sq.rearrange("p (h e) -> p h e", e=HD), AX, ALU.add).then_inc(s_yv, 1)

            def choose_experts(b, steps, part):
                def step(instruction):
                    instruction.then_inc(s_route, 1)
                    steps[0] += 1
                    dve.wait_ge(s_route, b * ROUTE_STEPS + steps[0])

                total, inverse, tiny = (small[:, i, :] for i in range(3))

                def mark(values, marked, width, count):
                    nc.vector.memset(tiny, 1e-20)
                    for j in range(TILES):
                        last = nc.vector.max(largest[:, j, :], values[:, j, 0:width])
                    step(last)
                    step(nc.vector.memset(largest[:, :, count:8], FILLER))
                    nc.vector.memset(tiny, 1e-20)
                    for j in range(TILES):
                        last = nc.vector.match_replace(marked[:, j, :], largest[:, j, :], values[:, j, :], MARK)
                    step(last)

                if part == 0:
                    wait(dve, s_score, b + 1)
                    s4 = score.rearrange("p (g e) -> p g e", e=4)
                    nc.vector.tensor_tensor(pairs[:, :, 0:3], s4[:, :, 0:3], s4[:, :, 1:4], ALU.add)
                    nc.vector.tensor_tensor(pairs[:, :, 3:5], s4[:, :, 0:2], s4[:, :, 2:4], ALU.add)
                    step(nc.vector.tensor_tensor(pairs[:, :, 5:6], s4[:, :, 0:1], s4[:, :, 3:4], ALU.add))
                    step(nc.vector.tensor_reduce(sums[:, :, 0:N_GROUP],
                                                 pairs[:, :, :].rearrange("p (t g) e -> p t g e", g=N_GROUP), AX, ALU.max))
                    mark(sums, group_marked, 8, TOPK_GROUP)
                    step(nc.vector.tensor_scalar(sums[:, :, 0:N_GROUP], group_marked[:, :, 0:N_GROUP],
                                                 MARK / 2 + FILLER / 2, None, ALU.is_lt))
                    step(nc.vector.tensor_tensor(kept[:, :, 0:EXPERTS].rearrange("p t (g e) -> p t g e", e=4),
                                                 score.rearrange("p (t g e) -> p t g e", g=N_GROUP, e=4),
                                                 sums[:, :, 0:N_GROUP].unsqueeze(3).broadcast_to([P, TILES, N_GROUP, 4]),
                                                 ALU.mult))
                else:
                    mark(kept, marked, EXPERTS, TOP_K)
                    chosen = kept[:, :, 0:EXPERTS]
                    step(nc.vector.scalar_tensor_tensor(chosen, marked[:, :, 0:EXPERTS], MARK / 2 + FILLER / 2,
                                                        score.rearrange("p (t e) -> p t e", e=EXPERTS), ALU.is_lt, ALU.mult))
                    step(nc.vector.tensor_reduce(total, chosen, AX, ALU.add))
                    step(nc.vector.tensor_tensor(total, total, tiny, ALU.add))
                    step(nc.vector.reciprocal(inverse, total))
                    step(nc.vector.scalar_tensor_tensor(
                        comb_all[:, bass.ds(b * (TILES * EXPERTS), TILES * EXPERTS)].rearrange("p (t e) -> p t e", e=EXPERTS),
                        chosen, ROUTED_SCALING, inverse.unsqueeze(2).broadcast_to([P, TILES, EXPERTS]), ALU.mult, ALU.mult))
                    assert steps[0] == ROUTE_STEPS, steps[0]

            nc.vector.memset(kept[:, :, EXPERTS:SLOTS], FILLER).then_inc(s_filled, 1)
            nc.vector.memset(sums[:, :, N_GROUP:], FILLER).then_inc(s_filled, 1)
            norm_rows(0)
            split_x(0)
            dve.wait_ge(s_tables, 48)
            dve.wait_ge(g.s_rope, 16)
            dve.wait_ge(s_filled, 2)
            rotate(0, s_kp, s_kr, s_ks, 2)
            norm_rows(1)
            keep_skip(0)
            rotate(0, s_qp, s_qr, s_qs, 0)
            split_x(1)
            expand_k(0)
            steps = [0]
            choose_experts(0, steps, 0)
            choose_experts(0, steps, 1)

            def body(b, last=False):
                steps = [0]
                carry_states(b)
                mask_scores(b, (0, 1))
                rotate(b + 1, s_kp, s_kr, s_ks, 2)
                if not last:
                    norm_rows(b + 2)
                mask_scores(b, (2,))
                choose_experts(b + 1, steps, 0)
                mask_scores(b, (3,))
                expand_k(b + 1)
                keep_skip(b + 1)
                rotate(b + 1, s_qp, s_qr, s_qs, 0)
                if not last:
                    split_x(b + 2)
                choose_experts(b + 1, steps, 1)
                variances(b)

            body(0)
            with dve.Fori(1, NB - 2) as b:
                body(b)
            body(NB - 2, True)
            carry_states(NB - 1)
            mask_scores(NB - 1, range(GROUPS))
            variances(NB - 1)

        @block.gpsimd
        def _(pool):
            def sum_k(b):
                wait(pool, s_ks, b + 1)
                wait(pool, s_ktr, b)
                wait(pool, s_kl16, b)
                nc.gpsimd.tensor_tensor(k_t, cosine, sine, ALU.add).then_inc(s_kt, 1)
                wait(pool, s_kp16, b + 1)
                wait(pool, s_kh, b)
                nc.gpsimd.tensor_tensor(k_16[:, 1, :], k_t, k_16[:, 0, :], ALU.subtract).then_inc(s_kl16, 1)

            def sum_q(b):
                wait(pool, s_qs, b + 1)
                wait(pool, s_y, b)
                nc.gpsimd.tensor_tensor(q_t, cosine, sine, ALU.add).then_inc(s_qt, 1)
                wait(pool, s_qp16, b + 1)
                wait(pool, s_sc, 4 * b)
                nc.gpsimd.tensor_tensor(q_16[:, 1, :], q_t, q_16[:, 0, :], ALU.subtract).then_inc(s_ql16, 1)

            def low_part_ff(b, k):
                wait(pool, s_ff_hi, 2 * b + k + 1)
                wait(pool, s_ffdn, 2 * b)
                nc.gpsimd.tensor_tensor(ff_lo[k], ff[k], ff_hi[k].bitcast(F32), ALU.subtract).then_inc(s_ff_lo, 1)

            def body(b):
                low_part_ff(b, 0)
                low_part_ff(b, 1)
                sum_k(b)
                sum_q(b)

            pool.wait_ge(s_tables, 48)
            body(0)
            with pool.Fori(1, NB) as b:
                body(b)


def combine(nc, sem, g):
    with ExitStack() as ctx:
        combine_in(nc, sem, g, lambda name, shape, dt=F32: ctx.enter_context(nc.sbuf_tensor(name, shape, dt)))


def combine_in(nc, sem, g, sb):
    NB, banks, late_raw = g.NB, g.banks, g.late_raw
    xn_all, y_all, skip_all = g.xn_all, g.y_all, g.skip_all
    comb_all, y_std, vec, ident = g.comb_all, g.y_var, g.vec, g.ident
    x_rows, out_rows = g.x_rows, g.out_rows

    def buffers(name, count, dt=F32):
        return [sb(f"{name}{i}", [P, T], dt)[:, :] for i in range(count)]

    n_first = N_UP - RMS_BLOCKS
    n_parts = n_first + N_SPLIT
    steps = [slice(a * P, b * P) for a, b in ((0, MOE - GATED), (MOE - GATED, n_first), (n_first, n_parts))]
    weights = [sb("late_w_hi", [P, n_parts * P], F32R), sb("late_w_lo", [P, n_parts * P], F32R)]
    router_raw = sb("router_raw", [P, 8 * P])
    router = sb("router", [P, 8 * P], F32R)
    x_t = buffers("x_t", 2, F32R)
    comb_t = sb("comb_t", [P, T], F32R)[:, :]
    yn, y_t, gated, y_gated, total, silu_ffn, product, x_in, result = buffers("c_rows", 9)
    act_out = buffers("act_out", 2)
    hidden = buffers("hidden", 2)
    hidden_hi = buffers("hidden_hi", 5, F32R)
    hidden_lo = buffers("hidden_lo", 5, F32R)
    comb_parts = sb("comb_parts", [P, TILES * 2 * EXPERTS])[:, :]
    y_rstd = sb("y_rstd", [P, TILES * HEADS])[:, :]
    N_MOE, N_SH = 8, 2
    N_BLK = N_MOE + N_SH
    U, B, O, G, YT, CT = 0, 2, 4, 5, 6, 7

    s_rt = sem("c_router_loaded")
    s_whi, s_wlo = sem("c_weights_high_part"), sem("c_weights_low_part")
    s_router = sem("c_router_ready")
    s_zero = sem("c_comb_t_zeroed")
    s_xhi, s_xlo = sem("c_x_hi"), sem("c_x_lo")
    s_cp = sem("c_comb_parts")
    s_ct = sem("c_comb_transposed")
    s_ctr = sem("c_comb_t_ready")
    s_rstd = sem("c_y_rstd")
    s_yn = sem("c_y_normed")
    s_ytr = sem("c_y_transposed")
    s_yt = sem("c_y_t_ready")
    s_gp = sem("c_gate_projected")
    s_gs = sem("c_gate_ready")
    s_yg = sem("c_y_gated")
    s_pr = sem("c_y_projected")
    s_tot = sem("c_branch_ready")
    s_up = sem("c_up_done")
    s_silu = sem("c_silu_ready")
    s_bc = sem("c_weights_spread")
    s_h = sem("c_hidden_weighted")
    s_hi = sem("c_hidden_high_part")
    s_lo = sem("c_hidden_low_part")
    s_dn = sem("c_down_done")
    s_g = sem("c_ffn_silu_ready")
    s_prod = sem("c_product_ready")
    s_bt = sem("c_product_by_rows")
    s_res = sem("c_result_ready")
    s_xin = sem("c_x_loaded")
    s_out = sem("c_out_stored")

    def sequences(engine, body, end=None):
        body(0, first=True)
        body(1)
        with engine.Fori(2, NB - 1) as b:
            body(b)
        body(NB - 1, last=True)
        if end is not None:
            end(NB - 1)

    with nc.Block() as block:
        @block.sync
        def _(sp):
            def store(b):
                wait(sp, s_res, b + 1)
                sp.dma_start(out_rows[:, bass.ds(b * TILES, TILES), :], result.rearrange("p (j c) -> p j c", c=P)
                             ).then_inc(s_out, 16)

            def body(b, first=False, last=False):
                if not first:
                    store(b - 1)
                sp.dma_start(x_in.rearrange("p (j c) -> p j c", c=P), x_rows[:, bass.ds(b * TILES, TILES), :]
                             ).then_inc(s_xin, 16)

            sp.dma_start(router_raw[:, :], g.t_router).then_inc(s_rt, 16)
            sequences(sp, body, store)
            sp.wait_ge(s_out, 16 * NB)

        @block.gpsimd
        def _(pool):
            def low_part(b, k):
                wait(pool, s_hi, b * N_BLK + k + 1)
                wait(pool, s_dn, b * N_BLK + k - 4)
                nc.gpsimd.tensor_tensor(hidden_lo[k % 5], hidden[k % 2], hidden_hi[k % 5].bitcast(F32),
                                        ALU.subtract).then_inc(s_lo, 1)

            def body(b, first=False, last=False):
                low_part(b, 0)
                low_part(b, 1)
                wait(pool, s_gs, b + 1)
                wait(pool, s_yt, b + 1)
                if not first:
                    wait(pool, s_pr, b)
                nc.gpsimd.tensor_tensor(y_gated, gated, y_t, ALU.mult).then_inc(s_yg, 1)
                for k in range(2, N_BLK):
                    low_part(b, k)

            sequences(pool, body)

        @block.tensor
        def _(pe):
            pe.wait_ge(s_wlo, 1)

            def by_rows(b):
                wait(pe, s_prod, b + 1)
                for j in range(TILES):
                    last = nc.tensor.transpose(banks[:, CT, j * P:(j + 1) * P], product[:, j * P:(j + 1) * P], ident[:, :])
                last.then_inc(s_bt, 1)

            def split_matmul(out, block, rhs):
                for i, (a, c) in enumerate(PARTS):
                    last = nc.tensor.matmul(out, weights[a][:, block * P:(block + 1) * P], rhs[c], start=i == 0, stop=i == 2)
                return last

            def block_up(b, k):
                wait(pe, s_silu, b * N_BLK + k - 1)
                split_matmul(banks[:, U + k % 2, :], SHARED - RMS_BLOCKS + k, x_t).then_inc(s_up, 1)

            def spread(b, first, m):
                if not (first and m < 2):
                    wait(pe, s_h, b * N_MOE + m - 1)
                nc.tensor.matmul(banks[:, B + m % 2, :], router[:, m * P:(m + 1) * P], comb_t,
                                 start=True, stop=True).then_inc(s_bc, 1)

            def block_down(b, k):
                wait(pe, s_lo, b * N_BLK + k + 1)
                at = n_first + (D_SHARED + k if k < N_SH else D_MOE + k - N_SH)
                rhs = (hidden_hi[k % 5], hidden_lo[k % 5])
                for i, (a, c) in enumerate(PARTS):
                    last = nc.tensor.matmul(banks[:, O, :], weights[a][:, at * P:(at + 1) * P], rhs[c],
                                            start=k == 0 and i == 0, stop=k == N_BLK - 1 and i == 2)
                last.then_inc(s_dn, 1)

            def last_blocks(b):
                block_down(b, N_BLK - 1)

            def body(b, first=False, last=False):
                wait(pe, s_xhi, b + 1)
                wait(pe, s_xlo, b + 1)
                block_up(b, 0)
                if not first:
                    block_down(b - 1, N_BLK - 2)
                block_up(b, 1)
                wait(pe, s_cp, 2 * b + 2)
                if not first:
                    wait(pe, s_res, b - 1)
                for j in range(TILES):
                    last = nc.tensor.transpose(banks[0:2 * EXPERTS, CT, j * P:(j + 1) * P],
                                               comb_parts[:, j * 2 * EXPERTS:(j + 1) * 2 * EXPERTS], ident[:, :])
                last.then_inc(s_ct, 1)
                if not first:
                    last_blocks(b - 1)
                    wait(pe, s_tot, b)
                split_matmul(banks[:, G, :], GATED - RMS_BLOCKS, x_t).then_inc(s_gp, 1)
                if first:
                    pe.wait_ge(s_wlo, 2)
                block_up(b, 2)
                wait(pe, s_ctr, b + 1)
                if first:
                    pe.wait_ge(s_router, 1)
                    pe.wait_ge(s_zero, 1)
                    pe.wait_ge(s_wlo, 3)
                spread(b, first, 0)
                wait(pe, s_yn, b + 1)
                if not first:
                    wait(pe, s_yt, b)
                for j in range(TILES):
                    last = nc.tensor.transpose(banks[:, YT, j * P:(j + 1) * P], yn[:, j * P:(j + 1) * P], ident[:, :])
                last.then_inc(s_ytr, 1)
                block_up(b, 3)
                spread(b, first, 1)
                if not first:
                    wait(pe, s_g, b)
                block_down(b, 0)
                if not first:
                    by_rows(b - 1)
                for k in range(4, N_BLK):
                    block_up(b, k)
                    block_down(b, k - 3)
                    spread(b, first, k - 2)
                wait(pe, s_yg, b + 1)
                nc.tensor.matmul(banks[:, G, :], late_raw[:, n_parts * P:], y_gated,
                                 start=True, stop=True).then_inc(s_pr, 1)
                block_down(b, N_BLK - 3)

            def end(b):
                block_down(b, N_BLK - 2)
                block_down(b, N_BLK - 1)
                by_rows(b)

            sequences(pe, body, end)

        @block.scalar
        def _(act):
            act.wait_ge(g.s_late, 48)
            nc.scalar.copy(weights[0][:, steps[0]], late_raw[:, steps[0]]).then_inc(s_whi, 1)
            nc.scalar.copy(x_t[0], xn_all[:, 0:T]).then_inc(s_xhi, 1)
            nc.scalar.copy(weights[0][:, steps[1]], late_raw[:, steps[1]]).then_inc(s_whi, 1)
            nc.scalar.copy(weights[0][:, steps[2]], late_raw[:, steps[2]]).then_inc(s_whi, 1)
            def block_silu(b, first, k):
                wait(act, s_up, b * N_BLK + k + 1)
                if k < N_SH:
                    wait(act, s_lo, b * N_BLK + k - 1)
                    nc.scalar.activation(hidden[k % 2], banks[:, U + k % 2, :], ACT.Silu).then_inc(s_silu, 1)
                else:
                    m = k - N_SH
                    if not (first and m < 2):
                        wait(act, s_h, b * N_MOE + m - 1)
                    nc.scalar.activation(act_out[m % 2], banks[:, U + k % 2, :], ACT.Silu).then_inc(s_silu, 1)

            def high_part(b, k):
                if k < N_SH:
                    wait(act, s_silu, b * N_BLK + k + 1)
                else:
                    wait(act, s_h, b * N_MOE + k - N_SH + 1)
                wait(act, s_dn, b * N_BLK + k - 4)
                nc.scalar.copy(hidden_hi[k % 5], hidden[k % 2]).then_inc(s_hi, 1)

            def x_high_part(b):
                wait(act, s_up, b * N_BLK)
                wait(act, s_gp, b)
                nc.scalar.copy(x_t[0], xn_all[:, bass.ds(b * T, T)]).then_inc(s_xhi, 1)

            def silu_of_sum(b):
                wait(act, s_dn, b * N_BLK + N_BLK)
                wait(act, s_prod, b)
                nc.scalar.activation(silu_ffn, banks[:, O, :], ACT.Silu).then_inc(s_g, 1)

            def body(b, first=False, last=False):
                if not first:
                    high_part(b - 1, N_BLK - 1)
                block_silu(b, first, 0)
                block_silu(b, first, 1)
                high_part(b, 0)
                wait(act, s_ct, b + 1)
                wait(act, s_bc, b * N_MOE)
                if first:
                    act.wait_ge(s_zero, 1)
                nc.scalar.copy(comb_t[0:2 * EXPERTS, :], banks[0:2 * EXPERTS, CT, :]).then_inc(s_ctr, 1)
                high_part(b, 1)
                if not first:
                    silu_of_sum(b - 1)
                wait(act, s_gp, b + 1)
                wait(act, s_yg, b)
                nc.scalar.activation(gated, banks[:, G, :], ACT.Silu, bias=vec[:, 3:4]).then_inc(s_gs, 1)
                block_silu(b, first, 2)
                wait(act, s_ytr, b + 1)
                nc.scalar.activation(y_t, banks[:, YT, :], ACT.Identity, bias=vec[:, 2:3], scale=vec[:, 1:2]).then_inc(s_yt, 1)
                for k in range(3, N_BLK):
                    if k == N_BLK - 1 and not last:
                        x_high_part(b + 1)
                    block_silu(b, first, k)
                    high_part(b, k - 1)

            def end(b):
                high_part(b, N_BLK - 1)
                silu_of_sum(b)

            sequences(act, body, end)

        @block.vector
        def _(dve):
            comb_halves = comb_parts.rearrange("p (j w e) -> p j w e", j=TILES, w=2)

            def low_part(part, count):
                dve.wait_ge(s_whi, count)
                nc.vector.tensor_tensor(weights[1][:, part], late_raw[:, part], weights[0][:, part].bitcast(F32),
                                        ALU.subtract).then_inc(s_wlo, 1)

            def x_low_part(b):
                wait(dve, s_xhi, b + 1)
                nc.vector.tensor_tensor(x_t[1], xn_all[:, bass.ds(b * T, T)], x_t[0].bitcast(F32),
                                        ALU.subtract).then_inc(s_xlo, 1)

            low_part(steps[0], 1)
            x_low_part(0)
            nc.vector.memset(comb_t.bitcast(F32), 0.0).then_inc(s_zero, 1)
            low_part(steps[1], 2)
            low_part(steps[2], 3)
            dve.wait_ge(s_rt, 16)
            nc.vector.tensor_copy(router[:, :], router_raw[:, :]).then_inc(s_router, 1)

            def add_branches(b):
                wait(dve, s_pr, b + 1)
                wait(dve, s_prod, b)
                nc.vector.tensor_tensor(total, banks[:, G, :], skip_all[:, bass.ds(b * T, T)],
                                        ALU.add).then_inc(s_tot, 1)

            def multiply(b):
                wait(dve, s_g, b + 1)
                wait(dve, s_tot, b + 1)
                wait(dve, s_bt, b)
                nc.vector.tensor_tensor(product, total, silu_ffn, ALU.mult).then_inc(s_prod, 1)

            def residual(b):
                wait(dve, s_bt, b + 1)
                wait(dve, s_xin, b * 16 + 16)
                wait(dve, s_out, b * 16)
                nc.vector.tensor_tensor(result, banks[:, CT, :], x_in, ALU.add).then_inc(s_res, 1)

            def body(b, first=False, last=False):
                if not first:
                    add_branches(b - 1)
                comb = comb_all[:, bass.ds(b * (TILES * EXPERTS), TILES * EXPERTS)].rearrange("p (j e) -> p j e", j=TILES)
                wait(dve, s_ct, b)
                nc.vector.tensor_copy(comb_halves[:, :, 0, :].bitcast(F32R), comb).then_inc(s_cp, 1)
                wait(dve, s_cp, 2 * b + 1)
                nc.vector.tensor_tensor(comb_halves[:, :, 1, :].bitcast(F32R), comb, comb_halves[:, :, 0, :],
                                        ALU.subtract).then_inc(s_cp, 1)
                wait(dve, s_yn, b)
                nc.vector.reciprocal(y_rstd, y_std[:, bass.ds(b * (TILES * HEADS), TILES * HEADS)]).then_inc(s_rstd, 1)
                wait(dve, s_rstd, b + 1)
                wait(dve, s_ytr, b)
                nc.vector.tensor_tensor(yn.rearrange("p (h e) -> p h e", e=HD),
                                        y_all[:, bass.ds(b * T, T)].rearrange("p (h e) -> p h e", e=HD),
                                        y_rstd.unsqueeze(2).broadcast_to([P, TILES * HEADS, HD]), ALU.mult).then_inc(s_yn, 1)
                if not first:
                    multiply(b - 1)
                for m in range(N_MOE):
                    k = m + N_SH
                    if m == N_MOE - 1 and not last:
                        x_low_part(b + 1)
                    wait(dve, s_silu, b * N_BLK + k + 1)
                    wait(dve, s_bc, b * N_MOE + m + 1)
                    wait(dve, s_lo, b * N_BLK + k - 1)
                    nc.vector.tensor_tensor(hidden[k % 2], act_out[m % 2], banks[:, B + m % 2, :],
                                            ALU.mult).then_inc(s_h, 1)
                    if m == 2 and not first:
                        residual(b - 1)

            def end(b):
                add_branches(b)
                multiply(b)
                residual(b)

            sequences(dve, body, end)


def kernel(**inputs):
    import numpy as _np
    import concourse.bacc as _bacc
    from concourse import mybir as _mybir
    from concourse.bass_utils import run_bass_kernel_spmd as _run

    a = {k.replace("L0_", ""): _np.asarray(v) for k, v in inputs.items()}
    C = 128
    qkvff = a["attn_w_qkvff"].T
    w_up = _np.concatenate([qkvff, a["attn_w_gated"].T, a["ffn_shared_up"],
                            a["ffn_expert_up"].transpose(1, 0, 2).reshape(C, -1)], 1)
    w_down = _np.concatenate([a["ffn_expert_down"].reshape(-1, C), a["ffn_shared_down"], a["attn_w_ff"].T,
                              a["attn_w_proj"].T], 0).reshape(-1, C, C).transpose(1, 0, 2).reshape(C, -1)
    vecs = _np.stack([a["attn_rms_w"], a["attn_gn_w"], a["attn_gn_b"], a["attn_b_gated"], a["attn_b_proj"]], 1)
    x = a["attn_x"]
    arrays = {"x": x.reshape(-1, C), "w_up": w_up, "w_down": w_down, "w_gate": a["ffn_gate_weight"].T, "vecs": vecs}
    arrays.update(shape_tables())
    arrays = {k: _np.ascontiguousarray(v) for k, v in arrays.items()}

    nc = _bacc.Bacc("TRN2", target_bir_lowering=False, num_devices=1)
    args = [nc.dram_tensor(k, v.shape, _mybir.dt.from_np(v.dtype), kind="ExternalInput").ap() for k, v in arrays.items()]
    out = nc.dram_tensor("out", arrays["x"].shape, _mybir.dt.from_np(_np.dtype("float32")), kind="ExternalOutput").ap()
    build(nc, *args, out)
    r = _run(nc, [arrays], core_ids=[0])
    return r.results[0]["out"].reshape(x.shape)
```
